# Optimizing a Trainium2 kernel written in Bass

```python
import numpy as np
import jax
import jax.numpy as jnp

def _softmax(x, axis=-1):
    return jax.nn.softmax(x, axis=axis)

def _gelu(x):
    return jax.nn.gelu(x, approximate=True)

def _silu(x):
    return jax.nn.silu(x)

def _sigmoid(x):
    return jax.nn.sigmoid(x)

def _layernorm(x, axis=-1, eps=1e-05):
    m = jnp.mean(x, axis=axis, keepdims=True)
    v = jnp.var(x, axis=axis, keepdims=True)
    return (x - m) / jnp.sqrt(v + eps)

def _scatter_add(tgt, idx, src, axis=0):
    return tgt.at[idx].add(src)

def _segment_sum(src, seg, n):
    return jax.ops.segment_sum(src, seg, n)
kernel_name = 'mk_decoder_preln_d2_seqx_r8_ea0880'

def setup_inputs(seed: int=0):
    np.random.seed(seed)
    _w = jnp.asarray

    def _rec_inputs():
        import jax
        import jax.numpy as jnp
        _rk = jax.random.key(seed)
        x = -0.0002928 + 1 * jax.random.normal(jax.random.fold_in(_rk, 1), (128, 64, 128), jnp.float32)
        _lenS = 64 - jax.random.randint(jax.random.fold_in(_rk, 7), (128,), 0, max(1, 64 // 4) + 1, jnp.int32)
        _lenS2 = 64 - jax.random.randint(jax.random.fold_in(_rk, 8), (128,), 0, max(1, 64 // 4) + 1, jnp.int32)
        _ctx_1024P = jax.random.normal(jax.random.fold_in(_rk, 11), (128, 16, 128), jnp.float32)
        _ctx_1024c = jax.random.dirichlet(jax.random.fold_in(_rk, 511), 0.3 * jnp.ones((16,), jnp.float32), (128, 64))
        _ctx_1024t = jnp.einsum('bsk,bkd->bsd', _ctx_1024c, _ctx_1024P)
        _ctx_1024t = _ctx_1024t * jax.lax.rsqrt(jnp.mean(jnp.square(_ctx_1024t)) + 1e-12) * 0.953939
        ctx_1024 = -1.39393e-06 + 0.999914 * (_ctx_1024t + 0.3 * jax.random.normal(jax.random.fold_in(_rk, 611), (128, 64, 128), jnp.float32))
        _validS = jnp.arange(64)[None, :] < _lenS[:, None]
        _validS2 = jnp.arange(64)[None, :] < _lenS2[:, None]
        _causal = jnp.tril(jnp.ones((64, 64), dtype=bool))
        mask_Bx1xSxS2_ik1 = jnp.where(jnp.broadcast_to(_validS2[:, None, None, :], (128, 1, 64, 64)), 1, 0).astype(jnp.int32)
        return (x, ctx_1024, mask_Bx1xSxS2_ik1)
    x, ctx_1024, mask_Bx1xSxS2_ik1 = _rec_inputs()

    def _L0_attn_setup():
        import jax, jax.numpy as jnp
        import numpy as np
        B, S, D, H = (4, 256, 128, 16)
        DH = D // H
        key = jax.random.key(seed)
        ks = jax.random.split(key, 6)
        scale = 1.0 / np.sqrt(D)
        return {'x': jax.random.normal(ks[0], (B, S, D), dtype=jnp.float32), 'Wq': jax.random.normal(ks[1], (D, D), dtype=jnp.float32) * scale, 'Wk': jax.random.normal(ks[2], (D, D), dtype=jnp.float32) * scale, 'Wv': jax.random.normal(ks[3], (D, D), dtype=jnp.float32) * scale, 'Wo': jax.random.normal(ks[4], (D, D), dtype=jnp.float32) * scale, 'rel_emb': jax.random.normal(ks[5], (2 * S - 1, DH), dtype=jnp.float32) * 0.02}
    _L0_attn_all = _L0_attn_setup()
    _L0_attn_in = {k: v for k, v in _L0_attn_all.items() if k in ('Wq', 'Wk', 'Wv', 'Wo', 'rel_emb')}
    del _L0_attn_all

    def _L0_xattn_setup():
        import jax, jax.numpy as jnp
        import numpy as np
        HIDDEN_DIM = 128
        NUM_HEADS = 16
        HEAD_DIM = HIDDEN_DIM // NUM_HEADS
        key = jax.random.key(seed)
        kq, kk, kv = jax.random.split(key, 3)
        shape = (2, 256, HIDDEN_DIM)
        return {'query': jax.random.normal(kq, shape, dtype=jnp.float32), 'key': jax.random.normal(kk, shape, dtype=jnp.float32), 'value': jax.random.normal(kv, shape, dtype=jnp.float32)}
    _L0_xattn_all = _L0_xattn_setup()
    _L0_xattn_in = {k: v for k, v in _L0_xattn_all.items() if k in ()}
    del _L0_xattn_all

    def _L0_ffn_setup():
        import jax, jax.numpy as jnp
        import numpy as np
        B, S, D, E, H, K = (4, 256, 128, 8, 256, 2)
        key = jax.random.key(seed)
        ks = jax.random.split(key, 9)
        scale = 0.02
        return {'da_input_thoughts': jax.random.normal(ks[0], (B, S, D), dtype=jnp.float32), 'Wr': jax.random.normal(ks[1], (D, E), dtype=jnp.float32) * scale, 'br': jnp.zeros((E,), jnp.float32), 'W1': jax.random.normal(ks[2], (E, D, H), dtype=jnp.float32) * scale, 'b1': jnp.zeros((E, H), jnp.float32), 'W2': jax.random.normal(ks[3], (E, H, H), dtype=jnp.float32) * scale, 'b2': jnp.zeros((E, H), jnp.float32), 'W3': jax.random.normal(ks[4], (E, H, D), dtype=jnp.float32) * scale, 'b3': jnp.zeros((E, D), jnp.float32)}
    _L0_ffn_all = _L0_ffn_setup()
    _L0_ffn_in = {k: v for k, v in _L0_ffn_all.items() if k in ('Wr', 'br', 'W1', 'b1', 'W2', 'b2', 'W3', 'b3')}
    del _L0_ffn_all

    def _L1_attn_setup():
        import jax, jax.numpy as jnp
        import numpy as np
        import math
        LN_EPS = 1e-05

        def _layernorm(h, gamma, beta):
            mu = jnp.mean(h, axis=-1, keepdims=True)
            var = jnp.var(h, axis=-1, keepdims=True)
            return (h - mu) * jax.lax.rsqrt(var + LN_EPS) * gamma + beta
        key = jax.random.key(seed)
        ks = jax.random.split(key, 6)
        B, S, D = (4, 512, 128)
        x = jax.random.normal(ks[0], (B, S, D), dtype=jnp.float32)
        W_omega = jax.random.normal(ks[1], (D, D), dtype=jnp.float32) / math.sqrt(D)
        b_omega = jnp.zeros((D,), dtype=jnp.float32)
        log_scale = jnp.full((D,), math.log(0.1), dtype=jnp.float32)
        ln_gamma = jnp.ones((4 * D,), dtype=jnp.float32)
        ln_beta = jnp.zeros((4 * D,), dtype=jnp.float32)
        W1 = jax.random.normal(ks[2], (2 * D, 4 * D), dtype=jnp.float32) / math.sqrt(4 * D)
        b1 = jnp.zeros((2 * D,), dtype=jnp.float32)
        W2 = jax.random.normal(ks[3], (D, 2 * D), dtype=jnp.float32) / math.sqrt(2 * D)
        b2 = jnp.zeros((D,), dtype=jnp.float32)
        return {'x': x, 'W_omega': W_omega, 'b_omega': b_omega, 'log_scale': log_scale, 'ln_gamma': ln_gamma, 'ln_beta': ln_beta, 'W1': W1, 'b1': b1, 'W2': W2, 'b2': b2}
    _L1_attn_all = _L1_attn_setup()
    _L1_attn_in = {k: v for k, v in _L1_attn_all.items() if k in ('W_omega', 'b_omega', 'log_scale', 'ln_gamma', 'ln_beta', 'W1', 'b1', 'W2', 'b2')}
    del _L1_attn_all

    def _L1_xattn_setup():
        import jax, jax.numpy as jnp
        import numpy as np
        import math
        HEAD = 16
        D_MODEL = 128
        HEAD_DIM = D_MODEL // HEAD
        B, S = (2, 256)
        key = jax.random.key(seed)
        ks = jax.random.split(key, 9)
        sc = 1.0 / math.sqrt(D_MODEL)
        return {'q': jax.random.normal(ks[0], (B, S, D_MODEL), dtype=jnp.float32), 'k': jax.random.normal(ks[1], (B, S, D_MODEL), dtype=jnp.float32), 'v': jax.random.normal(ks[2], (B, S, D_MODEL), dtype=jnp.float32), 'mask': jax.random.randint(ks[3], (B, 1, S, S), 0, 2, dtype=jnp.int32), 'wq': jax.random.normal(ks[4], (D_MODEL, D_MODEL), dtype=jnp.float32) * sc, 'wk': jax.random.normal(ks[5], (D_MODEL, D_MODEL), dtype=jnp.float32) * sc, 'wv': jax.random.normal(ks[6], (D_MODEL, D_MODEL), dtype=jnp.float32) * sc, 'wo': jax.random.normal(ks[7], (D_MODEL, D_MODEL), dtype=jnp.float32) * sc, 'bo': jax.random.normal(ks[8], (D_MODEL,), dtype=jnp.float32) * 0.01}
    _L1_xattn_all = _L1_xattn_setup()
    _L1_xattn_in = {k: v for k, v in _L1_xattn_all.items() if k in ('wq', 'wk', 'wv', 'wo', 'bo')}
    del _L1_xattn_all

    def _L1_ffn_setup():
        import jax, jax.numpy as jnp
        import numpy as np
        CAPACITY_FACTOR = 0.5
        key = jax.random.key(seed)
        ks = jax.random.split(key, 5)
        B, S, D, F = (4, 512, 128, 512)
        scale_in = 1.0 / np.sqrt(D)
        scale_ff = 1.0 / np.sqrt(F)
        return {'hidden_states': jax.random.normal(ks[0], (B, S, D), dtype=jnp.float32), 'w_router': jax.random.normal(ks[1], (D,), dtype=jnp.float32) * scale_in, 'W1': jax.random.normal(ks[2], (D, F), dtype=jnp.float32) * scale_in, 'b1': jnp.zeros((F,), dtype=jnp.float32), 'W2': jax.random.normal(ks[3], (F, D), dtype=jnp.float32) * scale_ff, 'b2': jnp.zeros((D,), dtype=jnp.float32)}
    _L1_ffn_all = _L1_ffn_setup()
    _L1_ffn_in = {k: v for k, v in _L1_ffn_all.items() if k in ('w_router', 'W1', 'b1', 'W2', 'b2')}
    del _L1_ffn_all
    return {'x': x, 'ctx_1024': ctx_1024, 'mask_Bx1xSxS2_ik1': mask_Bx1xSxS2_ik1, 'L0_attn_Wq': _L0_attn_in['Wq'], 'L0_attn_Wk': _L0_attn_in['Wk'], 'L0_attn_Wv': _L0_attn_in['Wv'], 'L0_attn_Wo': _L0_attn_in['Wo'], 'L0_attn_rel_emb': _L0_attn_in['rel_emb'], 'L0_ffn_Wr': _L0_ffn_in['Wr'], 'L0_ffn_br': _L0_ffn_in['br'], 'L0_ffn_W1': _L0_ffn_in['W1'], 'L0_ffn_b1': _L0_ffn_in['b1'], 'L0_ffn_W2': _L0_ffn_in['W2'], 'L0_ffn_b2': _L0_ffn_in['b2'], 'L0_ffn_W3': _L0_ffn_in['W3'], 'L0_ffn_b3': _L0_ffn_in['b3'], 'L1_attn_W_omega': _L1_attn_in['W_omega'], 'L1_attn_b_omega': _L1_attn_in['b_omega'], 'L1_attn_log_scale': _L1_attn_in['log_scale'], 'L1_attn_ln_gamma': _L1_attn_in['ln_gamma'], 'L1_attn_ln_beta': _L1_attn_in['ln_beta'], 'L1_attn_W1': _L1_attn_in['W1'], 'L1_attn_b1': _L1_attn_in['b1'], 'L1_attn_W2': _L1_attn_in['W2'], 'L1_attn_b2': _L1_attn_in['b2'], 'L1_xattn_wq': _L1_xattn_in['wq'], 'L1_xattn_wk': _L1_xattn_in['wk'], 'L1_xattn_wv': _L1_xattn_in['wv'], 'L1_xattn_wo': _L1_xattn_in['wo'], 'L1_xattn_bo': _L1_xattn_in['bo'], 'L1_ffn_w_router': _L1_ffn_in['w_router'], 'L1_ffn_W1': _L1_ffn_in['W1'], 'L1_ffn_b1': _L1_ffn_in['b1'], 'L1_ffn_W2': _L1_ffn_in['W2'], 'L1_ffn_b2': _L1_ffn_in['b2']}

def reference(x, ctx_1024, mask_Bx1xSxS2_ik1, L0_attn_Wq, L0_attn_Wk, L0_attn_Wv, L0_attn_Wo, L0_attn_rel_emb, L0_ffn_Wr, L0_ffn_br, L0_ffn_W1, L0_ffn_b1, L0_ffn_W2, L0_ffn_b2, L0_ffn_W3, L0_ffn_b3, L1_attn_W_omega, L1_attn_b_omega, L1_attn_log_scale, L1_attn_ln_gamma, L1_attn_ln_beta, L1_attn_W1, L1_attn_b1, L1_attn_W2, L1_attn_b2, L1_xattn_wq, L1_xattn_wk, L1_xattn_wv, L1_xattn_wo, L1_xattn_bo, L1_ffn_w_router, L1_ffn_W1, L1_ffn_b1, L1_ffn_W2, L1_ffn_b2):
    import jax
    import jax.numpy as jnp

    def _L0_attn_ref(x, Wq, Wk, Wv, Wo, rel_emb):
        import jax, jax.numpy as jnp
        import numpy as np
        B, S, D, H = (4, 256, 128, 16)
        DH = D // H
        b, s, d = x.shape
        h, dh = (H, DH)
        q = (x @ Wq).reshape(b, s, h, dh).transpose(0, 2, 1, 3)
        k = (x @ Wk).reshape(b, s, h, dh).transpose(0, 2, 1, 3)
        v = (x @ Wv).reshape(b, s, h, dh).transpose(0, 2, 1, 3)
        inv_sqrt_dh = 1.0 / np.sqrt(dh)
        scores = jnp.einsum('bhid,bhjd->bhij', q, k) * inv_sqrt_dh
        qr = jnp.einsum('bhid,rd->bhir', q, rel_emb) * inv_sqrt_dh
        idx = jnp.arange(s)[None, :] - jnp.arange(s)[:, None] + (s - 1)
        rel_bias = jnp.take_along_axis(qr, idx[None, None, :, :], axis=-1)
        attn = jax.nn.softmax(scores + rel_bias, axis=-1)
        out = jnp.einsum('bhij,bhjd->bhid', attn, v)
        out = out.transpose(0, 2, 1, 3).reshape(b, s, d)
        return out @ Wo

    def _L0_xattn_ref(query, key, value):
        import jax, jax.numpy as jnp
        import numpy as np
        HIDDEN_DIM = 128
        NUM_HEADS = 16
        HEAD_DIM = HIDDEN_DIM // NUM_HEADS
        B, S, _ = query.shape
        q = query.reshape(B, S, NUM_HEADS, HEAD_DIM).transpose(0, 2, 1, 3)
        k = key.reshape(B, S, NUM_HEADS, HEAD_DIM).transpose(0, 2, 1, 3)
        v = value.reshape(B, S, NUM_HEADS, HEAD_DIM).transpose(0, 2, 1, 3)
        scale = 1.0 / jnp.sqrt(jnp.asarray(HEAD_DIM, dtype=q.dtype))
        scores = jnp.einsum('bhqd,bhkd->bhqk', q, k) * scale
        attn = jax.nn.softmax(scores, axis=-1)
        out = jnp.einsum('bhqk,bhkd->bhqd', attn, v)
        return out.transpose(0, 2, 1, 3).reshape(B, S, HIDDEN_DIM)

    def _L0_ffn_ref(da_input_thoughts, Wr, br, W1, b1, W2, b2, W3, b3):
        import jax, jax.numpy as jnp
        import numpy as np
        B, S, D, E, H, K = (4, 256, 128, 8, 256, 2)
        x = da_input_thoughts
        n_experts = Wr.shape[1]
        logits = jnp.einsum('bsd,de->bse', x, Wr) + br
        probs = jax.nn.softmax(logits, axis=-1)
        top_w, top_i = jax.lax.top_k(probs, K)
        top_w = top_w / jnp.sum(top_w, axis=-1, keepdims=True)
        cw = jnp.sum(jax.nn.one_hot(top_i, n_experts, dtype=x.dtype) * top_w[..., None], axis=2)
        out = jnp.zeros_like(x)
        for e in range(n_experts):
            h = jnp.einsum('bsd,dh->bsh', x, W1[e]) + b1[e]
            h = jnp.einsum('bsh,hk->bsk', h, W2[e]) + b2[e]
            a = jax.nn.silu(h)
            y = jnp.einsum('bsh,hd->bsd', a, W3[e]) + b3[e]
            out = out + cw[..., e:e + 1] * y
        return out

    def _L1_attn_ref(x, W_omega, b_omega, log_scale, ln_gamma, ln_beta, W1, b1, W2, b2):
        import jax, jax.numpy as jnp
        import numpy as np
        import math
        LN_EPS = 1e-05

        def _layernorm(h, gamma, beta):
            mu = jnp.mean(h, axis=-1, keepdims=True)
            var = jnp.var(h, axis=-1, keepdims=True)
            return (h - mu) * jax.lax.rsqrt(var + LN_EPS) * gamma + beta
        B, S, D = x.shape
        omega = jnp.einsum('bsd,ed->bse', x, W_omega) + b_omega
        position = jnp.arange(1, S + 1, dtype=x.dtype).reshape(1, S, 1)
        pos_scale = 1.0 / jnp.sqrt(position)
        omega_scaled = omega * jnp.exp(log_scale) * pos_scale
        phi = jnp.cumsum(omega_scaled, axis=1)
        cos_phi = jnp.cos(phi)
        sin_phi = jnp.sin(phi)
        cm_real = x * cos_phi
        cm_imag = x * sin_phi
        mem_real = jnp.cumsum(cm_real, axis=1) / position
        mem_imag = jnp.cumsum(cm_imag, axis=1) / position
        ret_real = mem_real * cos_phi + mem_imag * sin_phi
        ret_imag = mem_imag * cos_phi - mem_real * sin_phi
        context = jnp.concatenate([cm_real, cm_imag, ret_real, ret_imag], axis=-1)
        h = _layernorm(context, ln_gamma, ln_beta)
        h = jnp.einsum('bsd,ed->bse', h, W1) + b1
        h = jax.nn.gelu(h, approximate=False)
        h = jnp.einsum('bsd,ed->bse', h, W2) + b2
        return x + h

    def _L1_xattn_ref(q, k, v, mask, wq, wk, wv, wo, bo):
        import jax, jax.numpy as jnp
        import numpy as np
        import math
        HEAD = 16
        D_MODEL = 128
        HEAD_DIM = D_MODEL // HEAD
        B, S = (2, 256)
        N, Lq, _ = q.shape
        Lk = k.shape[1]
        qh = (q @ wq).reshape(N, Lq, HEAD, HEAD_DIM)
        kh = (k @ wk).reshape(N, Lk, HEAD, HEAD_DIM)
        vh = (v @ wv).reshape(N, Lk, HEAD, HEAD_DIM)
        scores = jnp.einsum('nqha,nkha->nhqk', qh, kh)
        scores = jnp.where(mask == 0, jnp.float32(-10000000000.0), scores)
        attn = jax.nn.softmax(scores / math.sqrt(HEAD_DIM), axis=-1)
        out = jnp.einsum('nhqk,nkha->nqha', attn, vh).reshape(N, Lq, D_MODEL)
        return out @ wo + bo

    def _L1_ffn_ref(hidden_states, w_router, W1, b1, W2, b2):
        import jax, jax.numpy as jnp
        import numpy as np
        CAPACITY_FACTOR = 0.5
        'Mixture-of-Depths block: route top-k tokens through an FFN inner block,\n            scatter back with sigmoid router weights; bypassed tokens pass through.'
        B, S, D = hidden_states.shape
        k = int(S * CAPACITY_FACTOR)
        scores = jnp.einsum('bsd,d->bs', hidden_states, w_router)
        top_scores, top_idx = jax.lax.top_k(scores, k)
        weights = jax.nn.sigmoid(top_scores)
        selected = jnp.take_along_axis(hidden_states, top_idx[:, :, None], axis=1)
        h = jax.nn.gelu(jnp.einsum('bkd,df->bkf', selected, W1) + b1)
        processed = jnp.einsum('bkf,fd->bkd', h, W2) + b2
        update = weights[:, :, None] * processed

        def scatter_one(xb, ib, ub):
            return xb.at[ib].add(ub)
        output = jax.vmap(scatter_one)(hidden_states, top_idx, update)
        return output
    x = x + _L0_attn_ref(_layernorm(x, axis=-1), L0_attn_Wq, L0_attn_Wk, L0_attn_Wv, L0_attn_Wo, L0_attn_rel_emb)
    x = x + _L0_xattn_ref(_layernorm(x, axis=-1), ctx_1024, ctx_1024)
    x = x + _L0_ffn_ref(_layernorm(x, axis=-1), L0_ffn_Wr, L0_ffn_br, L0_ffn_W1, L0_ffn_b1, L0_ffn_W2, L0_ffn_b2, L0_ffn_W3, L0_ffn_b3)
    x = x + _L1_attn_ref(_layernorm(x, axis=-1), L1_attn_W_omega, L1_attn_b_omega, L1_attn_log_scale, L1_attn_ln_gamma, L1_attn_ln_beta, L1_attn_W1, L1_attn_b1, L1_attn_W2, L1_attn_b2)
    x = x + _L1_xattn_ref(_layernorm(x, axis=-1), ctx_1024, ctx_1024, mask_Bx1xSxS2_ik1, L1_xattn_wq, L1_xattn_wk, L1_xattn_wv, L1_xattn_wo, L1_xattn_bo)
    x = x + _L1_ffn_ref(_layernorm(x, axis=-1), L1_ffn_w_router, L1_ffn_W1, L1_ffn_b1, L1_ffn_W2, L1_ffn_b2)
    return x

_drawn_inputs = setup_inputs


def setup_inputs(seed=0):
    import zlib

    import numpy as np

    out = dict(_drawn_inputs(seed))
    spreads = {'L0_ffn_br': (0.0, 0.1),
     'L0_ffn_b1': (0.0, 0.8),
     'L0_ffn_b2': (0.0, 0.8),
     'L0_ffn_b3': (0.0, 0.345),
     'L1_attn_b_omega': (0.0, 0.432),
     'L1_attn_log_scale': (-2.3025851249694824, 0.2),
     'L1_attn_ln_gamma': (1.0, 0.2),
     'L1_attn_ln_beta': (0.0, 0.281),
     'L1_attn_b1': (0.0, 0.272),
     'L1_attn_b2': (0.0, 0.374),
     'L1_ffn_b1': (0.0, 0.8),
     'L1_ffn_b2': (0.0, 0.56)}
    factors = {'L0_attn_rel_emb': 8.0,
     'L0_ffn_W1': 7.624,
     'L0_ffn_W2': 7.126,
     'L0_ffn_W3': 4.659,
     'L1_xattn_bo': 24.684}
    for name, (base, spread) in spreads.items():
        noise = np.random.default_rng([zlib.crc32(name.encode()), seed]).standard_normal(out[name].shape)
        drawn = base * np.exp(spread * noise) if base else spread * noise
        out[name] = jnp.asarray(drawn.astype(out[name].dtype))
    for name, factor in factors.items():
        out[name] = (out[name] * factor).astype(out[name].dtype)
    return out
```

```python
import numpy as np
import concourse.bass as bass
from concourse import mybir
from contextlib import ExitStack

F32 = mybir.dt.float32
BF16 = mybir.dt.bfloat16
I32 = mybir.dt.int32
U32 = mybir.dt.uint32
ALU = mybir.AluOpType
ACT = mybir.ActivationFunctionType
AX = mybir.AxisListType

BATCH, SEQ, D = 128, 64, 128
HEADS = 16
DH = D // HEADS
PAIRS = HEADS // 2
PARTS = 128
TILES = BATCH * SEQ // PARTS
PER_CHUNK = 4
CHUNKS = TILES // PER_CHUNK
CTOK = PER_CHUNK * PARTS
CSEQ = 2 * PER_CHUNK
SCORES = PAIRS * 2 * SEQ
EXPERTS, HID = 8, 256
FF = 512
VCOL = DH + 1
VPAIR = 4 * VCOL
VWIN = 96
VBUF = (PAIRS - 1) * VPAIR + VWIN
VSLOTS = 4
REL = 2 * SEQ - 1
LN_EPS = 1e-5
CAP = -(2.0 ** 33)
BIG = 3.0e38
KEPT = SEQ // 2
SM_SCALE = float(1.0 / np.sqrt(DH))
TWO_PI = 2 * np.pi

C_ID, C_SWAP, C_NEG, C_DELTA, C_POS, C_INV, C_CHAIN, C_ONES, C_EIGHT, C_HEAD, C_END = np.cumsum(
    [0, 128, 128, 128, 32, 64, 64, 64, 128, 8, 2])


def constants():
    c = np.zeros((PARTS, C_END), np.float32)
    c[:, C_ID:C_ID + 128] = np.eye(PARTS)
    for p in range(PARTS):
        c[p, C_SWAP + (p ^ 32)] = 1.0
    for p in range(PARTS):
        if p % 64 < 32:
            c[p, C_NEG + 64 * (p // 64):C_NEG + 64 * (p // 64) + 64] = -1.0
    for p in range(PARTS):
        c[p, C_DELTA + p % 32] = 1.0
    pos = np.arange(1, SEQ + 1, dtype=np.float32)
    c[:, C_POS:C_POS + SEQ] = 1.0 / np.sqrt(pos)
    c[:, C_INV:C_INV + SEQ] = 1.0 / pos
    c[:, C_CHAIN:C_CHAIN + SEQ] = (np.arange(SEQ) > 0)
    c[:, C_ONES:C_ONES + 128] = 1.0 / (4 * D)
    c[:, C_EIGHT:C_EIGHT + 8] = 8 - np.arange(8)
    for p in range(PARTS):
        c[p, C_HEAD + (p // DH) % 2] = 1.0
    return c


def need(eng, sem, count):
    if isinstance(count, int) and count <= 0:
        return
    eng.wait_ge(sem, count)


def inside(n, count):
    return not isinstance(n, int) or 0 <= n < count


def sweep(eng, count, lead, lag, step, period=2):
    first = -(-(lag + 2) // period) * period
    rounds = (count - lead - first) // period
    for k in range(-lead, first):
        step(k, k % period)
    with eng.Fori(0, rounds) as r:
        for u in range(period):
            step(r * period + (first + u), u)
    for k in range(first + period * rounds, count + lag):
        step(k, k % period)


def repeat(eng, count, body):
    body(0)
    with eng.Fori(1, count) as n:
        body(n)


class Mem:

    def __init__(self, nc, stack, tag, g=None):
        self.nc, self.stack, self.tag, self.g = nc, stack, tag, g
        if g is not None:
            self.old, g.sems = g.sems, []
            stack.callback(self.release_old)

    def release_old(self):
        for sem in self.old:
            self.nc.release_semaphore(sem)

    def clear_old(self, engine):
        nums = sorted(sem.num for sem in self.old)
        for n in nums:
            if n - 1 not in nums:
                end = next(e for e in range(n + 1, 257) if e not in nums)
                engine.sem_clear(range(n, end))

    def sb(self, name, shape, dt=F32):
        return self.stack.enter_context(self.nc.sbuf_tensor(f"{self.tag}_{name}", list(shape), dt))

    def ps(self, name, shape, dt=F32):
        return self.stack.enter_context(self.nc.psum_tensor(f"{self.tag}_{name}", list(shape), dt))

    def sem(self, name):
        self.g.sems.append(self.nc.alloc_semaphore(f"{self.tag}_{name}"))
        return self.g.sems[-1]


def bc(ap, *shape):
    return ap.to_broadcast(list(shape))



def load_block(nc, g, io):
    with ExitStack() as stack:
        m = Mem(nc, stack, "load", g)
        pieces = 8
        s_const, s_stat = m.sem("constants_in"), m.sem("stats_done")
        s_x = [m.sem(f"x_in{n}") for n in range(pieces)]
        per = TILES // pieces
        with nc.Block() as block:
            @block.sync
            def _(sp):
                m.clear_old(sp)
                for q in range(pieces):
                    sp.dma_start(g.x[:, q * per:(q + 1) * per, :],
                                 io["x"][:, q * per:(q + 1) * per, :]).then_inc(s_x[q], 16)
                    if q == 0:
                        sp.dma_start(g.const[:], io["const"]).then_inc(s_const, 16)
                for q in range(pieces):
                    sp.wait_ge(s_x[q], 16)
                sp.wait_ge(s_const, 16)

            @block.vector
            def _(dve):
                for q in range(pieces):
                    dve.wait_ge(s_x[q], 16)
                    for t in range(q * per, (q + 1) * per):
                        nc.vector.bn_stats(g.stat[:, t, :], g.x[:, t, :]).then_inc(s_stat, 1)
                dve.wait_ge(s_const, 16)
                nc.vector.tensor_copy(g.swap[:], g.const[:, C_SWAP:C_SWAP + 128]).then_inc(s_stat, 1)
                nc.vector.tensor_copy(g.neg[:], g.const[:, C_NEG:C_NEG + 128]).then_inc(s_stat, 1)
                nc.vector.tensor_copy(g.delta[:], g.const[:, C_DELTA:C_DELTA + 32]).then_inc(s_stat, 1)


def norm_block(nc, g, tag):
    with ExitStack() as stack:
        m = Mem(nc, stack, tag, g)
        half = m.sb("half", [PARTS, TILES])
        sq = m.sb("sq", [PARTS, TILES])
        var = m.sb("var", [PARTS, TILES])
        s_v, s_var, s_root = m.sem("vector_step"), m.sem("variance"), m.sem("root")
        with nc.Block() as block:
            @block.sync
            def _(sp):
                m.clear_old(sp)

            @block.vector
            def _(dve):
                v = nc.vector
                even, odd = g.stat[:, :, 1], g.stat[:, :, 4]
                v.tensor_tensor(g.mean[:], even, odd, ALU.add).then_inc(s_v, 1)
                v.tensor_tensor(half[:], even, odd, ALU.subtract).then_inc(s_v, 1)
                v.tensor_tensor(var[:], g.stat[:, :, 2], g.stat[:, :, 5], ALU.add).then_inc(s_v, 1)
                dve.wait_ge(s_v, 3)
                v.tensor_scalar(g.mean[:], g.mean[:], 0.5, None, ALU.mult).then_inc(s_v, 1)
                v.tensor_tensor(sq[:], half[:], half[:], ALU.mult).then_inc(s_v, 1)
                v.tensor_scalar(var[:], var[:], 1.0 / D, LN_EPS, ALU.mult, ALU.add).then_inc(s_v, 1)
                dve.wait_ge(s_v, 6)
                v.scalar_tensor_tensor(var[:], sq[:], 0.25, var[:], ALU.mult, ALU.add).then_inc(s_var, 1)
                dve.wait_ge(s_root, 1)
                v.reciprocal(g.rstd[:], half[:]).then_inc(s_v, 1)

            @block.scalar
            def _(act):
                act.wait_ge(s_var, 1)
                nc.scalar.activation(half[:], var[:], ACT.Sqrt).then_inc(s_root, 1)



def project_block(nc, g, io, tag, wq=None, wk=None, wv=None, ctx=None):
    with ExitStack() as stack:
        m = Mem(nc, stack, tag, g)
        xn = m.sb("xn", [PARTS, 2, CTOK])
        src = m.sb("src", [PARTS, 2, CTOK])
        other = m.sb("ctx", [PARTS, 2, CTOK]) if ctx is not None and wk else None
        w = m.sb("w", [PARTS, 3, D])
        p_t = m.ps("p_t", [PARTS, 2, CTOK])
        p_q = m.ps("p_q", [PARTS, 2, CTOK])
        p_k = m.ps("p_k", [PARTS, 2, CTOK])
        p_v = m.ps("p_v", [PARTS, 2, CSEQ * D // 2])
        s_w, s_xn, s_tr, s_src = (m.sem(n) for n in (
            "weights_in", "xn_ready", "transposed", "src_ready"))
        s_ctx = [m.sem(f"ctx_in{n}") for n in range(2)]
        s_proj, s_v, s_out_q, s_out_v = (m.sem(n) for n in (
            "qk_done", "v_done", "qk_kept", "v_kept"))
        direct = wk is None
        with nc.Block() as block:
            @block.sync
            def _(sp):
                m.clear_old(sp)
                if direct:
                    for n in range(4):
                        w4 = BATCH * SEQ // 4
                        sp.dma_start(g.kt[:, n * w4:(n + 1) * w4],
                                     io["ctx_t"][:, n * w4:(n + 1) * w4]).then_inc(s_w, 16)
                    for hp in range(2):
                        sp.dma_start(g.v2[64 * hp:64 * hp + 64, :, :], io["ctx_v"][hp]).then_inc(s_w, 16)
                    sp.wait_ge(s_w, 96)
                    return
                for n, name in enumerate((wq, wk, wv)):
                    sp.dma_start(w[:, n, :], io[name]).then_inc(s_w, 16)
                if other is None:
                    return

                def step(k, par):
                    need(sp, s_v, k - 1)
                    sp.dma_start(other[:, par, :],
                                 io["ctx_t"][:, bass.ts(k, CTOK)]).then_inc(s_ctx[par], 16)
                sweep(sp, CHUNKS, 0, 0, step)

            @block.vector
            def _(dve):
                def step(k, par):
                    n = k + 2
                    if inside(n, CHUNKS):
                        need(dve, s_tr, n - 1)
                        for u in range(PER_CHUNK):
                            t = n * PER_CHUNK + u
                            nc.vector.tensor_scalar(
                                xn[:, par, u * D:(u + 1) * D], g.x[:, t, :],
                                g.mean[:, bass.ts(t, 1)], g.rstd[:, bass.ts(t, 1)],
                                ALU.subtract, ALU.mult).then_inc(s_xn, 1)
                    if not direct and inside(k, CHUNKS):
                        need(dve, s_v, k + 1)
                        nc.vector.tensor_copy(
                            g.v2[:, bass.ts(k, CSEQ), :].rearrange("p b c -> p (b c)"),
                            p_v[:, par, :]).then_inc(s_out_v, 1)
                sweep(dve, CHUNKS, 2, 0, step)

            @block.scalar
            def _(act):
                def step(k, par):
                    n = k + 1
                    if inside(n, CHUNKS):
                        need(act, s_tr, n + 1)
                        if direct:
                            nc.scalar.copy(g.qt[:, bass.ts(n, CTOK)], p_t[:, 1 - par, :]).then_inc(s_src, 1)
                        else:
                            need(act, s_v, n - 1)
                            nc.scalar.copy(src[:, 1 - par, :], p_t[:, 1 - par, :]).then_inc(s_src, 1)
                    if not direct and inside(k, CHUNKS):
                        need(act, s_proj, 2 * k + 1)
                        nc.scalar.copy(g.qt[:, bass.ts(k, CTOK)], p_q[:, par, :]).then_inc(s_out_q, 1)
                        need(act, s_proj, 2 * k + 2)
                        nc.scalar.copy(g.kt[:, bass.ts(k, CTOK)], p_k[:, par, :]).then_inc(s_out_q, 1)
                sweep(act, CHUNKS, 1, 0, step)

            @block.tensor
            def _(pe):
                if not direct:
                    pe.wait_ge(s_w, 48)

                def step(k, par):
                    n = k + 1
                    if inside(n, CHUNKS):
                        need(pe, s_src, n - 1)
                        need(pe, s_xn, PER_CHUNK * (n + 1))
                        for u in range(PER_CHUNK):
                            cols = slice(u * D, (u + 1) * D)
                            last = nc.tensor.transpose(p_t[:, 1 - par, cols], xn[:, 1 - par, cols],
                                                       g.const[:, C_ID:C_ID + 128])
                        last.then_inc(s_tr, 1)
                    if not direct and inside(k, CHUNKS):
                        keys = src if other is None else other
                        need(pe, s_src, k + 1)
                        need(pe, s_out_q, 2 * k - 3)
                        nc.tensor.matmul(p_q[:, par, :], w[:, 0, :], src[:, par, :],
                                         start=True, stop=True).then_inc(s_proj, 1)
                        if other is not None:
                            need(pe, s_ctx[par], (k - par) * 8 + 16)
                        need(pe, s_out_q, 2 * k - 2)
                        nc.tensor.matmul(p_k[:, par, :], w[:, 1, :], keys[:, par, :],
                                         start=True, stop=True).then_inc(s_proj, 1)
                        need(pe, s_out_v, k - 1)
                        for b in range(CSEQ):
                            for hp in range(2):
                                last = nc.tensor.matmul(
                                    p_v[64 * hp:64 * hp + 64, par, b * D // 2:(b + 1) * D // 2],
                                    keys[:, par, b * SEQ:(b + 1) * SEQ],
                                    w[:, 2, :].rearrange("p (h e d) -> p h e d", e=2, d=DH)[:, :, hp, :],
                                    start=True, stop=True, skip_group_check=True)
                        last.then_inc(s_v, 1)
                sweep(pe, CHUNKS, 1, 0, step)


def bias_block(nc, g, io):
    with ExitStack() as stack:
        m = Mem(nc, stack, "bias", g)
        GROUP = 4
        GROUPS = SEQ // GROUP
        rel = m.sb("rel", [PARTS, PAIRS, 2, REL])
        win = m.sb("win", [PARTS, 2, GROUP, 2, SEQ])
        keep = m.sb("keep", [PARTS, 2, BATCH, SEQ // 2])
        p_b = m.ps("p_b", [PARTS, 4, GROUP, BATCH])
        s_rel, s_win, s_bias, s_keep = (m.sem(n) for n in (
            "rel_in", "window_ready", "bias_done", "bias_kept"))
        s_out = [m.sem(f"bias_out{n}") for n in range(2)]
        q_at = g.qt[:].rearrange("p (b i) -> p b i", i=SEQ)
        with nc.Block() as block:
            @block.sync
            def _(sp):
                m.clear_old(sp)
                sp.dma_start(rel[:], io["rel"]).then_inc(s_rel, 16)

                def pair(h):
                    for half in range(2):
                        need(sp, s_keep, h * GROUPS + (half + 1) * GROUPS // 2)
                        sp.dma_start(g.bias_dram[:, bass.ds(h * 2 + half, 1), :, :],
                                     keep[:, half, :, :].rearrange("p (o b) i -> p o b i", o=1)
                                     ).then_inc(s_out[half], 16)
                repeat(sp, PAIRS, pair)
                for half in range(2):
                    sp.wait_ge(s_out[half], 16 * PAIRS)

            @block.vector
            def _(dve):
                dve.wait_ge(s_rel, 16)

                def pair(h):
                    for q in range(GROUPS):
                        need(dve, s_bias, h * GROUPS + q - 1)
                        for r in range(GROUP):
                            i = q * GROUP + r
                            nc.vector.tensor_copy(
                                win[:, q % 2, r, :, :],
                                rel[:, bass.ds(h, 1), :, SEQ - 1 - i:REL - i]
                                .rearrange("p o e j -> p (o e) j")).then_inc(s_win, 1)
                repeat(dve, PAIRS, pair)

            @block.tensor
            def _(pe):
                def pair(h):
                    for q in range(GROUPS):
                        need(pe, s_win, (h * GROUPS + q + 1) * GROUP)
                        need(pe, s_keep, h * GROUPS + q - 3)
                        for r in range(GROUP):
                            last = nc.tensor.matmul(
                                p_b[:, q % 4, r, :], win[:, q % 2, r, :, :],
                                q_at[:, :, q * GROUP + r], start=True, stop=True)
                        last.then_inc(s_bias, 1)
                repeat(pe, PAIRS, pair)

            @block.scalar
            def _(act):
                def pair(h):
                    for q in range(GROUPS):
                        if q % (GROUPS // 2) == 0:
                            need(act, s_out[q // (GROUPS // 2)], h * 16)
                        need(act, s_bias, h * GROUPS + q + 1)
                        i = (q * GROUP) % (SEQ // 2)
                        nc.scalar.copy(
                            keep[:, q // (GROUPS // 2), :, i:i + GROUP],
                            p_b[:, q % 4, :, :].rearrange("p r b -> p b r")).then_inc(s_keep, 1)
                repeat(act, PAIRS, pair)


def core_block(nc, g, io, tag, wo=None, bo=None, bias=False, mask=None):
    with ExitStack() as stack:
        m = Mem(nc, stack, tag, g)
        qm = m.sb("qm", [PARTS, 2, 4, PAIRS * SEQ])
        kst = m.sb("kst", [PARTS, 2, 4, PARTS])
        top = m.sb("top", [PARTS, 2, 32], BF16)
        top2 = m.sb("top2", [PARTS, 2, 32], BF16)
        spread = m.sb("spread", [PARTS, 2, 32, 32], BF16)
        prob = m.sb("prob", [PARTS, 2, PAIRS, 2, SEQ])
        vb = m.sb("vb", [PARTS, VSLOTS, VBUF])
        rsum = m.sb("rsum", [PARTS, 2, PAIRS, 2])
        on = m.sb("on", [PARTS, 2, D])
        p_s = m.ps("p_s", [PARTS, 2, 2, PAIRS * SEQ])
        p_o = m.ps("p_o", [PARTS, 512])
        p_m = m.ps("p_m", [PARTS, 512])
        p_t = m.ps("p_t", [PARTS, 512])
        p_w = m.ps("p_w", [PARTS, 512])
        s_clear, s_zero, s_w = (m.sem(n) for n in ("first_cleared", "cleared", "weights_in"))
        s_q = [m.sem(f"q_in{n}") for n in range(2)]
        s_kst = m.sem("keys_ready")
        s_extra = [m.sem(f"bias_or_mask_in{n}") for n in range(2)]
        s_sc, s_adj, s_top, s_swap, s_top2, s_spread, s_shift, s_prob = (m.sem(n) for n in (
            "scores_done", "scores_adjusted", "half_max", "swapped", "max_ready", "spread_ready",
            "shifted", "probs_ready"))
        s_vb, s_av, s_rs, s_on, s_ot, s_otk, s_y, s_x, s_stat, s_cap = (m.sem(n) for n in (
            "values_ready", "av_done", "sums_inverted", "out_normed", "out_transposed",
            "out_t_kept", "projected", "x_added", "stats_done", "cap_ready"))
        if wo:
            ot = m.sb("ot", [PARTS, 2, D])
            w = m.sb("w", [PARTS, D])
        if bo:
            bow = m.sb("bo", [1, D])
            one = m.sb("one", [1, PARTS])
        if bias:
            bt = m.sb("bt", [PARTS, 2, PAIRS * 2, 4, SEQ // 2])
        if mask:
            mt = m.sb("mt", [PARTS, 2, 4, SEQ], I32)
            cap0 = m.sb("cap0", [PARTS, 2, 2, SEQ])
            cap = m.sb("cap", [PARTS, 2, 2, SEQ])
        GROUPS = TILES // 2
        adjusts = 2 if bias or mask else 0
        SHIFT_AT, SWAP_AT = (3, PAIRS) if bias or mask else (2, 4)
        with nc.Block() as block:
            @block.sync
            def _(sp):
                m.clear_old(sp)
                if wo:
                    sp.dma_start(w[:], io[wo]).then_inc(s_w, 16)
                if bo:
                    sp.dma_start(bow[:], io[bo]).then_inc(s_w, 16)
                sp.wait_ge(s_zero, 1)

                def group(n, par):
                    need(sp, s_sc, 2 * (n - 1))
                    cols = bass.ts(n, 4 * SEQ)
                    for h in range(PAIRS):
                        rows = slice(2 * h * DH, 2 * (h + 1) * DH)
                        sp.dma_start(qm[rows, par, :, h * SEQ:(h + 1) * SEQ],
                                     g.qt[rows, cols].rearrange("p (b i) -> p b i", i=SEQ)
                                     ).then_inc(s_q[par], 16)
                    if bias:
                        need(sp, s_adj, adjusts * 2 * (n - 1))
                        sp.dma_start(bt[:, par, :, :, :],
                                     g.bias_dram[:, :, bass.ds(n * 4, 4), :]).then_inc(s_extra[par], 16)
                    if mask:
                        need(sp, s_cap, 2 * 2 * (n - 1))
                        sp.dma_start(mt[:, par, :, :],
                                     io[mask][:, bass.ds(n * 4, 4), :]).then_inc(s_extra[par], 16)
                sweep(sp, GROUPS, 0, 0, group)

            @block.gpsimd
            def _(pool):
                def step(k, ph):
                    par = ph % 2
                    if inside(k, TILES):
                        need(pool, s_top2, k + 1)
                        need(pool, s_shift, k - 1)
                        need(pool, s_vb, 2 * (k + 1))
                        nc.gpsimd.tensor_tensor(
                            spread[:, par, :, :],
                            bc(top2[:, par, :].rearrange("p (n o) -> p n o", o=1), PARTS, 32, 32),
                            bc(g.delta[:].rearrange("p (o c) -> p o c", o=1), PARTS, 32, 32),
                            ALU.mult).then_inc(s_spread, 1)
                    n = k + 1
                    if inside(n, TILES):
                        need(pool, s_av, n - VSLOTS + 1)
                        need(pool, s_spread, n)
                        for hp in range(2):
                            need(pool, s_vb, 2 * n + hp)
                            rows = slice(64 * hp, 64 * hp + 64)
                            nc.gpsimd.tensor_copy(
                                vb[rows, (ph + 1) % VSLOTS, 0:PAIRS * VPAIR].rearrange(
                                    "p (h b e d) -> p b h e d", h=PAIRS, b=2, e=2)[:, :, :, hp, 0:DH],
                                g.v2[rows, bass.ds(n * 2, 2), :].rearrange(
                                    "p b (h d) -> p b h d", d=DH)).then_inc(s_vb, 1)
                pool.wait_ge(s_zero, 2)
                sweep(pool, TILES, 1, 0, step, 4)

            @block.vector
            def _(dve):
                v = nc.vector
                v.memset(qm[:], 0.0).then_inc(s_zero, 1)
                v.memset(vb[:], 0.0).then_inc(s_clear, 1)
                dve.wait_ge(s_clear, 1)
                for hp in range(2):
                    last = v.memset(vb[64 * hp:64 * hp + 64, :, 0:PAIRS * VPAIR].rearrange(
                        "p s (n e d) -> p s n e d", e=2, d=VCOL)[:, :, :, hp, DH], 1.0)
                last.then_inc(s_zero, 1)
                if bo:
                    v.memset(one[:], 1.0).then_inc(s_zero, 1)

                def step(k, ph):
                    par = ph % 2
                    n = k + 1
                    if inside(n, TILES):
                        slot, sub = 1 - par, (ph + 1) % 2
                        gs = ((ph + 1) // 2) % 2
                        if mask:
                            if sub == 0:
                                need(dve, s_extra[gs], (n - 2 * gs) * 4 + 16)
                            v.tensor_scalar(cap0[:, slot, :, :], mt[:, gs, 2 * sub:2 * sub + 2, :],
                                            0, BIG - CAP, ALU.not_equal, ALU.mult).then_inc(s_cap, 1)
                            need(dve, s_cap, 2 * n + 1)
                            v.tensor_scalar(cap[:, slot, :, :], cap0[:, slot, :, :],
                                            CAP, None, ALU.add).then_inc(s_cap, 1)
                            need(dve, s_cap, 2 * n + 2)
                        need(dve, s_sc, n + 1)
                        for b in range(adjusts):
                            sc = p_s[:, slot, b, :].rearrange("p (h i) -> p h i", i=SEQ)
                            if mask:
                                v.tensor_tensor(sc, sc, bc(cap[:, slot, b:b + 1, :], PARTS, PAIRS, SEQ),
                                                ALU.min).then_inc(s_adj, 1)
                            else:
                                if b == 0 and sub == 0:
                                    need(dve, s_extra[gs], (n - 2 * gs) * 4 + 16)
                                sc = p_s[:, slot, b, :].rearrange("p (h c) -> p h c", c=SEQ // 2)
                                v.tensor_tensor(sc, sc, bt[:, gs, :, 2 * sub + b, :],
                                                ALU.add).then_inc(s_adj, 1)
                        if adjusts:
                            need(dve, s_adj, (n + 1) * adjusts)
                        v.tensor_reduce(
                            top[:, slot, :],
                            p_s[:, slot, :, :].rearrange("p b (n c) -> p (b n) c", c=32),
                            AX.X, ALU.max, apply_transpose=True).then_inc(s_top, 1)
                        need(dve, s_swap, n + 1)
                        need(dve, s_spread, n - 1)
                        v.tensor_tensor(top2[:, slot, :], top[:, slot, :],
                                        p_m[:, 0:32], ALU.max).then_inc(s_top2, 1)
                    n = k - 1
                    if inside(n, TILES):
                        slot = 1 - par
                        need(dve, s_av, n + 1)
                        for b in range(2):
                            rows = slice(64 * b, 64 * b + 64)
                            o = p_o[rows, 0:PAIRS * VPAIR].rearrange(
                                "p (h b e d) -> p h b e d", h=PAIRS, b=2, e=2)
                            v.reciprocal(rsum[rows, slot, :, :], o[:, :, b, :, DH]).then_inc(s_rs, 1)
                        need(dve, s_rs, 2 * (n + 1))
                        if wo:
                            need(dve, s_ot, n - 1)
                        for b in range(2):
                            rows = slice(64 * b, 64 * b + 64)
                            o = p_o[rows, 0:PAIRS * VPAIR].rearrange(
                                "p (h b e d) -> p h b e d", h=PAIRS, b=2, e=2)
                            v.tensor_tensor(
                                on[rows, slot, :].rearrange("p (h e d) -> p h e d", e=2, d=DH),
                                o[:, :, b, :, 0:DH],
                                bc(rsum[rows, slot, :, :].rearrange("p h (e o) -> p h e o", o=1),
                                   64, PAIRS, 2, DH), ALU.mult).then_inc(s_on, 1)
                    n = k - 3 if wo else k - 1
                    if inside(n, TILES):
                        xt = g.x[:, bass.ds(n, 1), :].rearrange("p o d -> p (o d)")
                        slot = 1 - par
                        if wo:
                            need(dve, s_y, n + 1)
                            v.tensor_tensor(xt, xt, p_w[:, 0:D],
                                            ALU.add).then_inc(s_x, 1)
                        else:
                            need(dve, s_on, 2 * (n + 1))
                            v.tensor_tensor(xt, xt, on[:, slot, :], ALU.add).then_inc(s_x, 1)
                    n = k - 3
                    if inside(n, TILES):
                        need(dve, s_x, n + 1)
                        v.bn_stats(g.stat[:, bass.ds(n, 1), :].rearrange("p o c -> p (o c)"),
                                   g.x[:, bass.ds(n, 1), :].rearrange("p o d -> p (o d)")
                                   ).then_inc(s_stat, 1)
                sweep(dve, TILES, 1, 3, step, 4)

            @block.scalar
            def _(act):
                def step(k, ph):
                    par = ph % 2
                    if inside(k, TILES):
                        need(act, s_shift, k + 1)
                        need(act, s_av, k - 1)
                        nc.scalar.activation(
                            prob[:, par, :, :, :].rearrange("p h b i -> p b h i"),
                            p_s[:, par, :, :].rearrange("p b (h i) -> p b h i", i=SEQ),
                            ACT.Exp, scale=SM_SCALE).then_inc(s_prob, 1)
                    n = k + 2
                    if par == 0 and inside(n, TILES):
                        need(act, s_sc, n - 2)
                        for hp in range(2):
                            nc.scalar.activation(
                                kst[:, (ph // 2 + 1) % 2, :, SEQ * hp:SEQ * hp + SEQ],
                                g.kt[:, bass.ds(n * 2 * SEQ, 4 * SEQ)].rearrange(
                                    "p (b j) -> p b j", j=SEQ),
                                ACT.Identity, scale=g.const[:, C_HEAD + hp:C_HEAD + hp + 1]
                                ).then_inc(s_kst, 1)
                    n = k - 2
                    if wo and inside(n, TILES):
                        need(act, s_ot, n + 1)
                        need(act, s_y, n - 1)
                        nc.scalar.copy(ot[:, par, :], p_t[:, 0:D]).then_inc(s_otk, 1)
                sweep(act, TILES, 2, 2, step, 4)

            @block.tensor
            def _(pe):
                mm = nc.tensor.matmul
                if wo:
                    pe.wait_ge(s_w, 32 if bo else 16)
                pe.wait_ge(s_zero, 3 if bo else 2)

                def step(k, ph):
                    par = ph % 2
                    n = k + 1
                    if inside(n, TILES):
                        slot, sub = 1 - par, (ph + 1) % 2
                        gs = ((ph + 1) // 2) % 2
                        if sub == 0:
                            loads = 16 * PAIRS
                            need(pe, s_q[gs], (n - 2 * gs) * (loads // 4) + loads)
                            need(pe, s_kst, n + 2)
                        need(pe, s_prob, n - 1)
                        for b in range(2):
                            bi = 2 * sub + b
                            last = mm(p_s[:, slot, b, :], kst[:, gs, bi, :], qm[:, gs, bi, :],
                                      start=True, stop=True, skip_group_check=True)
                        last.then_inc(s_sc, 1)
                    def weigh(heads):
                        if not inside(k - 1, TILES):
                            return
                        if heads and heads[0] == 0:
                            need(pe, s_prob, k)
                            need(pe, s_vb, 2 * k)
                            need(pe, s_on, 2 * (k - 1))
                        for h in heads:
                            last = mm(p_o[:, VPAIR * h:VPAIR * h + VWIN],
                                      prob[:, 1 - par, h, :, :],
                                      vb[:, (ph - 1) % VSLOTS, VPAIR * h:VPAIR * h + VWIN],
                                      start=True, stop=True, skip_group_check=True)
                        if heads and heads[-1] == PAIRS - 1:
                            last.then_inc(s_av, 1)
                    def swap():
                        n = k + 1
                        if not inside(n, TILES):
                            return
                        slot = 1 - par
                        need(pe, s_top, n + 1)
                        need(pe, s_top2, n)
                        mm(p_m[:, 0:32], g.swap[:], top[:, slot, :],
                           start=True, stop=True, skip_group_check=True).then_inc(s_swap, 1)
                    weigh(range(SHIFT_AT))
                    if inside(k, TILES):
                        need(pe, s_spread, k + 1)
                        for b in range(2):
                            last = mm(p_s[:, par, b, :], g.neg[:],
                                      spread[:, par, 16 * b:16 * b + 16, :].rearrange(
                                          "p n c -> p (n c)"),
                                      start=False, stop=True, skip_group_check=True)
                        last.then_inc(s_shift, 1)
                    weigh(range(SHIFT_AT, SWAP_AT))
                    if SWAP_AT < PAIRS:
                        swap()
                    weigh(range(SWAP_AT, PAIRS))
                    n = k - 2
                    if wo and inside(n, TILES):
                        need(pe, s_on, 2 * (n + 1))
                        need(pe, s_otk, n)
                        nc.tensor.transpose(p_t[:, 0:D], on[:, par, :],
                                            g.const[:, C_ID:C_ID + 128]).then_inc(s_ot, 1)
                    n = k - 3
                    if wo and inside(n, TILES):
                        slot = 1 - par
                        y = p_w[:, 0:D]
                        need(pe, s_otk, n + 1)
                        need(pe, s_x, n)
                        last = mm(y, ot[:, slot, :], w[:], start=True, stop=not bo,
                                  skip_group_check=True)
                        if bo:
                            last = mm(y, one[:], bow[:], start=False, stop=True,
                                      skip_group_check=True)
                        last.then_inc(s_y, 1)
                    if SWAP_AT == PAIRS:
                        swap()
                sweep(pe, TILES, 1, 3, step, 4)



def norm_chunk(nc, g, xn, n, sem):
    for u in range(PER_CHUNK):
        t = n * PER_CHUNK + u
        nc.vector.tensor_scalar(xn[:, u * D:(u + 1) * D], g.x[:, t, :], g.mean[:, bass.ts(t, 1)],
                                g.rstd[:, bass.ts(t, 1)], ALU.subtract, ALU.mult).then_inc(sem, 1)


def experts_block(nc, g, io):
    with ExitStack() as stack:
        m = Mem(nc, stack, "moe", g)
        w1t = m.sb("w1t", [PARTS, EXPERTS, 2, D])
        w2 = m.sb("w2", [PARTS, EXPERTS, 2, HID])
        b1c = m.sb("b1c", [PARTS, EXPERTS, 2])
        b2c = m.sb("b2c", [PARTS, EXPERTS * 2])
        w12 = m.sb("w12", [PARTS, EXPERTS, HID])
        b12 = m.sb("b12", [PARTS, EXPERTS * 2])
        w3 = m.sb("w3", [PARTS, EXPERTS, 2, D])
        b3 = m.sb("b3", [EXPERTS, D])
        wr = m.sb("wr", [PARTS, EXPERTS])
        br = m.sb("br", [PARTS, EXPERTS])
        xn = m.sb("xn", [PARTS, 2, CTOK])
        xt = m.sb("xt", [PARTS, 2, CTOK])
        act_t = m.sb("act_t", [PARTS, 2, 2, CTOK])
        cwt = m.sb("cwt", [EXPERTS, CTOK])
        small = [PARTS, PER_CHUNK, EXPERTS]
        lg, eq, pick, hot1, hot2, rest = (m.sb(n, small) for n in (
            "lg", "eq", "pick", "hot1", "hot2", "rest"))
        cw = m.sb("cw", [PARTS, 2] + small[1:])
        best, best2, first, gap, wt1, wt2 = (m.sb(n, [PARTS, PER_CHUNK]) for n in (
            "best", "best2", "first", "gap", "wt1", "wt2"))
        p_t = m.ps("p_t", [PARTS, CTOK])
        p_l = m.ps("p_l", [PARTS, 512])
        p_h = m.ps("p_h", [PARTS, 2, 2, CTOK])
        p_y = m.ps("p_y", [PARTS, 2, PER_CHUNK, D])
        s_w, s_w12, s_w12k, s_b12, s_b12k = (m.sem(n) for n in (
            "weights_in", "w12_done", "w12_kept", "b12_done", "b12_kept"))
        s_xn, s_tr, s_xt, s_lg, s_r, s_gap, s_wt, s_cw = (m.sem(n) for n in (
            "xn_ready", "transposed", "xt_ready", "logits_done", "router_step", "gap_ready",
            "pair_weights", "cw_ready"))
        s_hot = m.sem("hot_weighted")
        s_ct, s_ctk, s_b3, s_init, s_h, s_a, s_y, s_acc, s_stat = (m.sem(n) for n in (
            "cw_transposed", "cwt_ready", "b3_done", "x_started", "hidden_done", "act_ready",
            "expert_done", "accumulated", "stats_done"))
        ident = g.const[:, C_ID:C_ID + 128]
        names = ("moe_w1t", "moe_w2", "moe_b1", "moe_b2", "moe_w3", "moe_b3", "moe_wr", "moe_br")
        with nc.Block() as block:
            @block.sync
            def _(sp):
                m.clear_old(sp)
                for name, to in zip(names, (w1t, w2, b1c, b2c, w3, b3, wr, br)):
                    sp.dma_start(to[:], io[name]).then_inc(s_w, 16)
                sp.wait_ge(s_w, 16 * len(names))

            @block.tensor
            def _(pe):
                mm = nc.tensor.matmul
                pe.wait_ge(s_w, 16 * len(names))
                for e in range(EXPERTS):
                    need(pe, s_w12k, e - 1)
                    for hb in range(2):
                        last = mm(p_h[:, e % 2, 0, 0:HID], w1t[:, e, hb, :], w2[:, e, hb, :],
                                  start=(hb == 0), stop=(hb == 1))
                    last.then_inc(s_w12, 1)
                    for kb in range(2):
                        for hb in range(2):
                            last = mm(p_l[:, 2 * e + kb:2 * e + kb + 1],
                                      w2[:, e, hb, kb * D:(kb + 1) * D], b1c[:, e, hb:hb + 1],
                                      start=(hb == 0), stop=(hb == 1))
                last.then_inc(s_b12, 1)
                pe.wait_ge(s_w12k, EXPERTS)
                pe.wait_ge(s_b12k, 1)

                def step(k, par):
                    n = k + 1

                    def hidden(e):
                        if e == 0:
                            need(pe, s_xt, k + 1)
                        for hb in range(2):
                            need(pe, s_a, k * 2 * EXPERTS + 2 * e + hb - 3)
                            mm(p_h[:, e % 2, hb, :], w12[:, e, hb * D:(hb + 1) * D],
                               xt[:, par, :], start=True, stop=True).then_inc(s_h, 1)

                    def output(e):
                        need(pe, s_a, k * 2 * EXPERTS + 2 * e + 2)
                        need(pe, s_acc, k * EXPERTS + e - 1)
                        for u in range(PER_CHUNK):
                            for hb in range(2):
                                last = mm(p_y[:, e % 2, u, :], act_t[:, e % 2, hb, u * D:(u + 1) * D],
                                          w3[:, e, hb, :], start=(hb == 0), stop=(hb == 1))
                        last.then_inc(s_y, 1)

                    if inside(k, CHUNKS):
                        hidden(0)
                        hidden(1)
                        output(0)
                    if inside(n, CHUNKS):
                        need(pe, s_xn, PER_CHUNK * (n + 1))
                        need(pe, s_init, n)
                        for u in range(PER_CHUNK):
                            last = nc.tensor.transpose(p_t[:, u * D:(u + 1) * D],
                                                       xn[:, 1 - par, u * D:(u + 1) * D], ident)
                        last.then_inc(s_tr, 1)
                    if inside(k, CHUNKS):
                        hidden(2)
                        output(1)
                    if inside(n, CHUNKS):
                        need(pe, s_xt, n + 1)
                        need(pe, s_ctk, n)
                        for u in range(PER_CHUNK):
                            last = mm(p_l[:, u * EXPERTS:(u + 1) * EXPERTS],
                                      xt[:, 1 - par, u * D:(u + 1) * D], wr[:], start=True, stop=True)
                        last.then_inc(s_lg, 1)
                    if inside(k, CHUNKS):
                        for e in range(2, EXPERTS - 1):
                            hidden(e + 1)
                            output(e)
                    if inside(n, CHUNKS):
                        need(pe, s_cw, n + 1)
                        for u in range(PER_CHUNK):
                            last = nc.tensor.transpose(p_l[0:EXPERTS, u * D:(u + 1) * D],
                                                       cw[:, 1 - par, u, :], ident)
                        last.then_inc(s_ct, 1)
                    if inside(k, CHUNKS):
                        output(EXPERTS - 1)
                    if inside(n, CHUNKS):
                        need(pe, s_ctk, n + 1)
                        for u in range(PER_CHUNK):
                            last = mm(p_t[:, u * D:(u + 1) * D], cwt[:, u * D:(u + 1) * D], b3[:],
                                      start=True, stop=True)
                        last.then_inc(s_b3, 1)
                sweep(pe, CHUNKS, 1, 0, step)

            @block.scalar
            def _(act):
                for e in range(EXPERTS):
                    act.wait_ge(s_w12, e + 1)
                    nc.scalar.copy(w12[:, e, :], p_h[:, e % 2, 0, 0:HID]).then_inc(s_w12k, 1)

                def step(k, par):
                    n = k + 1

                    def silu(e):
                        need(act, s_y, k * EXPERTS + e - 1)
                        for hb in range(2):
                            need(act, s_h, k * 2 * EXPERTS + 2 * e + hb + 1)
                            nc.scalar.activation(act_t[:, e % 2, hb, :], p_h[:, e % 2, hb, :],
                                                 ACT.Silu, bias=b12[:, 2 * e + hb:2 * e + hb + 1]
                                                 ).then_inc(s_a, 1)
                    if inside(k, CHUNKS):
                        if isinstance(k, int) and k == 0:
                            act.wait_ge(s_b12k, 1)
                        silu(0)
                        silu(1)
                    if inside(n, CHUNKS):
                        need(act, s_tr, n + 1)
                        nc.scalar.copy(xt[:, 1 - par, :], p_t[:]).then_inc(s_xt, 1)
                    if inside(k, CHUNKS):
                        for e in range(2, 5):
                            silu(e)
                    if inside(n, CHUNKS):
                        for sign, to in ((-1.0, wt1), (1.0, wt2)):
                            need(act, s_gap, n + 1)
                            nc.scalar.activation(to[:], gap[:], ACT.Sigmoid, scale=sign
                                                 ).then_inc(s_wt, 1)
                    if inside(k, CHUNKS):
                        for e in range(5, EXPERTS):
                            silu(e)
                    if inside(n, CHUNKS):
                        need(act, s_ct, n + 1)
                        nc.scalar.copy(cwt[:], p_l[0:EXPERTS, :]).then_inc(s_ctk, 1)
                sweep(act, CHUNKS, 1, 0, step)

            @block.vector
            def _(dve):
                v = nc.vector
                dve.wait_ge(s_b12, 1)
                v.tensor_tensor(b12[:], p_l[:, 0:2 * EXPERTS], b2c[:], ALU.add).then_inc(s_b12k, 1)

                shape = (PARTS, PER_CHUNK, EXPERTS)
                wide = lambda a: bc(a.rearrange("p (u o) -> p u o", o=1), *shape)

                def step(k, par):
                    n = k + 1
                    if inside(n, CHUNKS):
                        need(dve, s_tr, n - 1)
                        norm_chunk(nc, g, xn[:, 1 - par, :], n, s_xn)

                    def accumulate(e):
                        need(dve, s_y, k * EXPERTS + e + 1)
                        need(dve, s_acc, k * EXPERTS + e)
                        for u in range(PER_CHUNK):
                            xt_ = g.x[:, k * PER_CHUNK + u, :]
                            last = v.scalar_tensor_tensor(xt_, p_y[:, e % 2, u, :],
                                                          cw[:, par, u, e:e + 1], xt_,
                                                          ALU.mult, ALU.add)
                        last.then_inc(s_acc, 1)

                    if inside(k, CHUNKS):
                        need(dve, s_b3, k + 1)
                        xc = g.x[:, bass.ts(k, PER_CHUNK), :].rearrange("p u d -> p (u d)")
                        v.tensor_tensor(xc, xc, p_t[:], ALU.add).then_inc(s_init, 1)
                        need(dve, s_init, k + 1)
                        accumulate(0)
                        accumulate(1)
                    if inside(n, CHUNKS):
                        R = 12
                        at = [0]

                        def then(ins):
                            at[0] += 1
                            ins.then_inc(s_r, 1)
                            need(dve, s_r, n * R + at[0])
                        order = bc(g.const[:, C_EIGHT:C_EIGHT + 8].rearrange("p (o e) -> p o e", o=1),
                                   *shape)
                        need(dve, s_lg, n + 1)
                        then(v.tensor_tensor(lg[:], p_l[:, 0:PER_CHUNK * EXPERTS].rearrange(
                            "p (u e) -> p u e", e=EXPERTS),
                            bc(br[:].rearrange("p (o e) -> p o e", o=1), *shape), ALU.add))

                        def top(values, top_, hot):
                            then(v.tensor_reduce(top_[:], values[:], AX.X, ALU.max))
                            then(v.tensor_tensor(eq[:], values[:], wide(top_[:]), ALU.is_equal))
                            then(v.tensor_tensor(pick[:], eq[:], order, ALU.mult))
                            then(v.tensor_reduce(first[:], pick[:], AX.X, ALU.max))
                            then(v.tensor_tensor(hot[:], pick[:], wide(first[:]), ALU.is_equal))
                        top(lg, best, hot1)
                        then(v.scalar_tensor_tensor(rest[:], hot1[:], -BIG, lg[:], ALU.mult, ALU.add))
                        top(rest, best2, hot2)
                        v.tensor_tensor(gap[:], best2[:], best[:], ALU.subtract).then_inc(s_gap, 1)
                    if inside(k, CHUNKS):
                        for e in range(2, EXPERTS - 2):
                            accumulate(e)
                    if inside(n, CHUNKS):
                        need(dve, s_wt, 2 * (n + 1))
                        v.tensor_tensor(hot1[:], hot1[:], wide(wt1[:]), ALU.mult).then_inc(s_hot, 1)
                        v.tensor_tensor(hot2[:], hot2[:], wide(wt2[:]), ALU.mult).then_inc(s_hot, 1)
                        need(dve, s_hot, 2 * (n + 1))
                        v.tensor_tensor(cw[:, 1 - par, :, :], hot1[:], hot2[:], ALU.add).then_inc(s_cw, 1)
                    if inside(k, CHUNKS):
                        for e in range(EXPERTS - 2, EXPERTS):
                            accumulate(e)
                        need(dve, s_acc, (k + 1) * EXPERTS)
                        for u in range(PER_CHUNK):
                            t = k * PER_CHUNK + u
                            v.bn_stats(g.stat[:, t, :], g.x[:, t, :]).then_inc(s_stat, 1)
                sweep(dve, CHUNKS, 1, 0, step)



MAGIC = 1.5 * 2.0 ** 23
TURN_HI = 6.28125
TURN_MID = float(np.float32(2 * np.pi - 6.28125))
TURN_LO = float(2 * np.pi - 6.28125 - np.float64(np.float32(2 * np.pi - 6.28125)))
PI = float(np.nextafter(np.float32(np.pi), np.float32(0)))


def memory_block(nc, g, io):
    with ExitStack() as stack:
        m = Mem(nc, stack, "mem", g)
        wo = m.sb("wo", [PARTS, D])
        lsc, bom = m.sb("lsc", [PARTS, 1]), m.sb("bom", [PARTS, 1])
        rate, shift = m.sb("rate", [PARTS, 1]), m.sb("shift", [PARTS, 1])
        gamma, beta = m.sb("gamma", [PARTS, 4]), m.sb("beta", [PARTS, 4])
        w1 = m.sb("w1", [PARTS, 4, 2 * D])
        w1g = m.sb("w1g", [PARTS, 4, 2 * D])
        wmean = m.sb("wmean", [PARTS, 2 * D])
        b1, h0 = m.sb("b1", [PARTS, 2]), m.sb("h0", [PARTS, 2])
        w2 = m.sb("w2", [PARTS, 2, D])
        b2 = m.sb("b2", [PARTS, D])
        chain = m.sb("chain", [PARTS, CSEQ, SEQ])
        xn = m.sb("xn", [PARTS, 4, CTOK])
        xt = m.sb("xt", [PARTS, 2, CTOK])
        oms = m.sb("oms", [PARTS, 2, CTOK])
        om, phi, t0, t1, y0, y1, sin, half, cos = (m.sb(n, [PARTS, CTOK]) for n in (
            "om", "phi", "t0", "t1", "y0", "y1", "sin", "half", "cos"))
        ctx = m.sb("ctx", [PARTS, 2, 4, CTOK])
        mem = m.sb("mem", [PARTS, 2, CTOK])
        prod = m.sb("prod", [PARTS, 4, CTOK])
        sqr = m.sb("sqr", [PARTS, 4, CTOK])
        m2, var, root, rinv = (m.sb(n, [PARTS, CTOK]) for n in ("m2", "var", "root", "rinv"))
        hn = m.sb("hn", [PARTS, 2, CTOK])
        gel = m.sb("gel", [PARTS, 2, CTOK])
        xb = m.sb("xb", [PARTS, CTOK])
        p_t = m.ps("p_t", [PARTS, CTOK])
        p_o = m.ps("p_o", [PARTS, CTOK])
        p_m = m.ps("p_m", [PARTS, CTOK])
        p_q = m.ps("p_q", [PARTS, CTOK])
        p_h = m.ps("p_h", [PARTS, 2, CTOK])
        p_y = m.ps("p_y", [PARTS, CTOK])
        S = {n: m.sem(n) for n in (
            "weights_in", "rate", "prep", "w1g", "wsums", "xn", "transposed", "xt", "omega",
            "om", "oms", "phi", "turns", "reduced", "sin", "half", "half_sq", "cos", "cm",
            "sums", "mem", "prod", "ret", "squares", "stat_sums", "mean_sq", "var", "root", "rinv",
            "hidden", "scaled", "gelu", "out", "xb", "x0", "x", "stats")}
        ident = g.const[:, C_ID:C_ID + 128]
        mean_of = g.const[:, C_ONES:C_ONES + 128]
        loads = ((wo, "mem_wo"), (lsc, "mem_ls"), (bom, "mem_bo"), (gamma, "mem_gamma"),
                 (beta, "mem_beta"), (w1, "mem_w1"), (b1, "mem_b1"), (w2, "mem_w2"), (b2, "mem_b2"))
        by_seq = lambda a: a.rearrange("p (b i) -> p b i", i=SEQ)
        per_pos = lambda c: bc(g.const[:, c:c + SEQ].rearrange("p (o i) -> p o i", o=1),
                               PARTS, CSEQ, SEQ)
        with nc.Block() as block:
            @block.sync
            def _(sp):
                m.clear_old(sp)
                for to, name in loads:
                    sp.dma_start(to[:], io[name]).then_inc(S["weights_in"], 16)
                sp.wait_ge(S["weights_in"], 16 * len(loads))

            @block.tensor
            def _(pe):
                mm = nc.tensor.matmul
                pe.wait_ge(S["weights_in"], 16 * len(loads))
                for e in range(2):
                    for f in range(4):
                        last = mm(p_y[:, e:e + 1], w1[:, f, e * D:(e + 1) * D], beta[:, f:f + 1],
                                  start=(f == 0), stop=(f == 3))
                last.then_inc(S["wsums"], 1)
                pe.wait_ge(S["w1g"], 4)
                for f in range(4):
                    last = mm(p_m[:, 0:2 * D], mean_of, w1g[:, f, :], start=(f == 0), stop=(f == 3))
                last.then_inc(S["wsums"], 1)
                pe.wait_ge(S["prep"], 8)

                def step(k, ph):
                    n = k + 2
                    if inside(n, CHUNKS):
                        need(pe, S["xn"], PER_CHUNK * (n + 1))
                        need(pe, S["xt"], n)
                        for u in range(PER_CHUNK):
                            last = nc.tensor.transpose(p_t[:, u * D:(u + 1) * D],
                                                       xn[:, (ph + 2) % 4, u * D:(u + 1) * D], ident)
                        last.then_inc(S["transposed"], 1)
                    if inside(n, CHUNKS):
                        need(pe, S["xt"], n + 1)
                        need(pe, S["om"], n)
                        mm(p_o[:], wo[:], xt[:, ph % 2, :], start=True, stop=True).then_inc(S["omega"], 1)
                    if inside(k, CHUNKS):
                        c = ctx[:, ph % 2, :, :]
                        need(pe, S["ret"], 2 * (k + 1))
                        need(pe, S["mean_sq"], k)
                        for f in range(4):
                            last = mm(p_m[:], mean_of, c[:, f, :], start=(f == 0), stop=(f == 3))
                        last.then_inc(S["stat_sums"], 1)
                    j = k - 1
                    if inside(j, CHUNKS):
                        need(pe, S["gelu"], 2 * (j + 1))
                        need(pe, S["x"], j)
                        for u in range(PER_CHUNK):
                            for e in range(2):
                                last = mm(p_y[:, u * D:(u + 1) * D], gel[:, e, u * D:(u + 1) * D],
                                          w2[:, e, :], start=(e == 0), stop=(e == 1))
                        last.then_inc(S["out"], 1)
                    if inside(k, CHUNKS):
                        need(pe, S["squares"], 4 * (k + 1))
                        need(pe, S["var"], k)
                        for f in range(4):
                            last = mm(p_q[:], mean_of, sqr[:, f, :], start=(f == 0), stop=(f == 3))
                        last.then_inc(S["stat_sums"], 1)
                        for e in range(2):
                            need(pe, S["scaled"], 2 * k - 1 + e)
                            for f in range(4):
                                last = mm(p_h[:, e, :], w1g[:, f, e * D:(e + 1) * D], c[:, f, :],
                                          start=(f == 0), stop=(f == 3))
                            last.then_inc(S["hidden"], 1)
                sweep(pe, CHUNKS, 2, 1, step, 4)

            @block.scalar
            def _(act):
                A = nc.scalar.activation
                act.wait_ge(S["weights_in"], 16 * len(loads))
                A(rate[:], lsc[:], ACT.Exp).then_inc(S["rate"], 1)
                act.wait_ge(S["prep"], 8)

                def step(k, ph):
                    n = k + 2
                    if inside(n, CHUNKS):
                        need(act, S["transposed"], n + 1)
                        need(act, S["cm"], 2 * (n - 1))
                        need(act, S["omega"], n - 1)
                        nc.scalar.copy(xt[:, ph % 2, :], p_t[:]).then_inc(S["xt"], 1)
                        need(act, S["omega"], n + 1)
                        need(act, S["oms"], n)
                        A(om[:], p_o[:], ACT.Identity, scale=rate[:], bias=shift[:]).then_inc(S["om"], 1)
                    j = k - 1
                    if inside(k, CHUNKS):
                        need(act, S["ret"], 2 * (k + 1))
                        need(act, S["stat_sums"], 2 * k)
                        for f in range(4):
                            A(sqr[:, f, :], ctx[:, ph % 2, f, :], ACT.Square).then_inc(S["squares"], 1)
                    n = k + 1
                    if inside(n, CHUNKS):
                        need(act, S["reduced"], n + 1)
                        need(act, S["cm"], 2 * n)
                        need(act, S["prod"], 4 * n)
                        A(sin[:], y1[:], ACT.Sin).then_inc(S["sin"], 1)
                        A(half[:], y1[:], ACT.Sin, scale=0.5).then_inc(S["half"], 1)
                        need(act, S["half"], n + 1)
                        need(act, S["cos"], n)
                        A(cos[:], half[:], ACT.Square).then_inc(S["half_sq"], 1)
                    if inside(k, CHUNKS):
                        need(act, S["stat_sums"], 2 * k + 1)
                        need(act, S["var"], k)
                        A(m2[:], p_m[:], ACT.Square).then_inc(S["mean_sq"], 1)
                        need(act, S["var"], k + 1)
                        need(act, S["rinv"], k)
                        A(root[:], var[:], ACT.Sqrt).then_inc(S["root"], 1)
                    if inside(k, CHUNKS):
                        for e in range(2):
                            need(act, S["scaled"], 2 * k + e + 1)
                            need(act, S["out"], k)
                            A(gel[:, e, :], hn[:, e, :], ACT.Gelu, bias=h0[:, e:e + 1]
                              ).then_inc(S["gelu"], 1)
                sweep(act, CHUNKS, 2, 0, step, 2)

            @block.gpsimd
            def _(pool):
                tt = nc.gpsimd.tensor_tensor
                pool.wait_ge(S["weights_in"], 16 * len(loads))

                def step(k, ph):
                    n = k + 2
                    if inside(n, CHUNKS):
                        need(pool, S["om"], n + 1)
                        need(pool, S["phi"], n - 1)
                        tt(by_seq(oms[:, ph % 2, :]), by_seq(om[:]), per_pos(C_POS), ALU.mult
                           ).then_inc(S["oms"], 1)
                    n = k + 1
                    if inside(n, CHUNKS):
                        c = ctx[:, (ph + 1) % 2, :, :]
                        for f in range(2):
                            need(pool, S["sums"], 2 * n + f + 1)
                            tt(by_seq(mem[:, f, :]), by_seq(mem[:, f, :]), per_pos(C_INV), ALU.mult
                               ).then_inc(S["mem"], 1)
                        need(pool, S["mem"], 2 * (n + 1))
                        need(pool, S["ret"], 2 * n)
                        for f, wave in enumerate((sin, cos)):
                            tt(prod[:, 2 + f, :], mem[:, f, :], wave[:], ALU.mult
                               ).then_inc(S["prod"], 1)
                    if inside(k, CHUNKS):
                        need(pool, S["x"], k)
                        tt(xb[:].rearrange("p (u d) -> p u d", d=D),
                           xn[:, ph % 4, :].rearrange("p (u d) -> p u d", d=D),
                           bc(b2[:].rearrange("p (o d) -> p o d", o=1), PARTS, PER_CHUNK, D),
                           ALU.add).then_inc(S["xb"], 1)
                sweep(pool, CHUNKS, 2, 0, step, 4)

            @block.vector
            def _(dve):
                v = nc.vector
                dve.wait_ge(S["weights_in"], 16 * len(loads))
                for f in range(4):
                    v.tensor_scalar(w1g[:, f, :], w1[:, f, :], gamma[:, f:f + 1], None, ALU.mult
                                    ).then_inc(S["w1g"], 1)
                v.tensor_copy(chain[:], per_pos(C_CHAIN)).then_inc(S["prep"], 1)
                dve.wait_ge(S["rate"], 1)
                v.tensor_tensor(shift[:], bom[:], rate[:], ALU.mult).then_inc(S["prep"], 1)
                dve.wait_ge(S["wsums"], 2)
                v.tensor_tensor(h0[:], p_y[:, 0:2], b1[:], ALU.add).then_inc(S["prep"], 1)
                v.tensor_copy(wmean[:], p_m[:, 0:2 * D]).then_inc(S["prep"], 1)
                dve.wait_ge(S["prep"], 4)
                dve.wait_ge(S["w1g"], 4)
                for f in range(4):
                    v.tensor_tensor(w1g[:, f, :], w1g[:, f, :], wmean[:], ALU.subtract
                                    ).then_inc(S["prep"], 1)

                def step(k, ph):
                    n = k + 1
                    if inside(n, CHUNKS):
                        need(dve, S["oms"], n + 1)
                        v.tensor_tensor_scan(phi[:], chain[:].rearrange("p b i -> p (b i)"),
                                             oms[:, (ph + 1) % 2, :],
                                             0.0, ALU.mult, ALU.add).then_inc(S["phi"], 1)
                        need(dve, S["phi"], n + 1)
                        v.tensor_scalar(t0[:], phi[:], 1.0 / TWO_PI, MAGIC, ALU.mult, ALU.add
                                        ).then_inc(S["turns"], 1)
                        need(dve, S["turns"], 5 * n + 1)
                        v.tensor_scalar(t1[:], t0[:], MAGIC, None, ALU.subtract
                                        ).then_inc(S["turns"], 1)
                        need(dve, S["turns"], 5 * n + 2)
                        v.scalar_tensor_tensor(y0[:], t1[:], -TURN_HI, phi[:], ALU.mult, ALU.add
                                               ).then_inc(S["turns"], 1)
                        need(dve, S["turns"], 5 * n + 3)
                        v.scalar_tensor_tensor(t0[:], t1[:], -TURN_MID, y0[:], ALU.mult, ALU.add
                                               ).then_inc(S["turns"], 1)
                        need(dve, S["turns"], 5 * n + 4)
                        v.scalar_tensor_tensor(y0[:], t1[:], -TURN_LO, t0[:], ALU.mult, ALU.add
                                               ).then_inc(S["turns"], 1)
                        need(dve, S["turns"], 5 * n + 5)
                        v.tensor_scalar(y1[:], y0[:], -PI, PI, ALU.max, ALU.min
                                        ).then_inc(S["reduced"], 1)
                    if inside(n, CHUNKS):
                        c = ctx[:, (ph + 1) % 2, :, :]
                        need(dve, S["half_sq"], n + 1)
                        v.tensor_scalar(cos[:], cos[:], -2.0, 1.0, ALU.mult, ALU.add
                                        ).then_inc(S["cos"], 1)
                        need(dve, S["cos"], n + 1)
                        need(dve, S["sin"], n + 1)
                        need(dve, S["hidden"], 2 * (n - 1))
                        for f, wave in enumerate((cos, sin)):
                            v.tensor_tensor(c[:, f, :], xt[:, (ph + 1) % 2, :], wave[:], ALU.mult
                                            ).then_inc(S["cm"], 1)
                            need(dve, S["cm"], 2 * n + f + 1)
                            need(dve, S["ret"], 2 * n)
                            v.tensor_tensor_scan(
                                mem[:, f, :], chain[:].rearrange("p b i -> p (b i)"), c[:, f, :],
                                0.0, ALU.mult, ALU.add).then_inc(S["sums"], 1)
                    if inside(k + 3, CHUNKS):
                        need(dve, S["xb"], k)
                        norm_chunk(nc, g, xn[:, (ph + 3) % 4, :], k + 3, S["xn"])
                    j = k - 2
                    if inside(j, CHUNKS):
                        need(dve, S["x"], j + 1)
                        for u in range(PER_CHUNK):
                            t = j * PER_CHUNK + u
                            v.bn_stats(g.stat[:, t, :], g.x[:, t, :]).then_inc(S["stats"], 1)
                    if inside(k, CHUNKS):
                        need(dve, S["stat_sums"], 2 * k + 2)
                        need(dve, S["mean_sq"], k + 1)
                        need(dve, S["root"], k)
                        v.scalar_tensor_tensor(var[:], p_q[:], LN_EPS, m2[:], ALU.add, ALU.subtract
                                               ).then_inc(S["var"], 1)
                        need(dve, S["root"], k + 1)
                        v.reciprocal(rinv[:], root[:]).then_inc(S["rinv"], 1)
                        need(dve, S["rinv"], k + 1)
                    if inside(n, CHUNKS):
                        need(dve, S["mem"], 2 * (n + 1))
                        v.tensor_tensor(prod[:, 0, :], mem[:, 0, :], cos[:], ALU.mult
                                        ).then_inc(S["prod"], 1)
                        v.tensor_tensor(prod[:, 1, :], mem[:, 1, :], sin[:], ALU.mult
                                        ).then_inc(S["prod"], 1)
                        need(dve, S["prod"], 4 * (n + 1))
                        v.tensor_tensor(c[:, 2, :], prod[:, 0, :], prod[:, 1, :], ALU.add
                                        ).then_inc(S["ret"], 1)
                        v.tensor_tensor(c[:, 3, :], prod[:, 3, :], prod[:, 2, :], ALU.subtract
                                        ).then_inc(S["ret"], 1)
                    if inside(k, CHUNKS):
                        for e in range(2):
                            need(dve, S["hidden"], 2 * k + e + 1)
                            need(dve, S["gelu"], 2 * k - 1 + e)
                            v.tensor_tensor(hn[:, e, :], p_h[:, e, :], rinv[:], ALU.mult
                                            ).then_inc(S["scaled"], 1)
                    j = k - 1
                    if inside(j, CHUNKS):
                        xc = g.x[:, bass.ts(j, PER_CHUNK), :].rearrange("p u d -> p (u d)")
                        need(dve, S["xb"], j + 1)
                        need(dve, S["out"], j + 1)
                        v.tensor_tensor(y0[:], p_y[:], xb[:], ALU.add).then_inc(S["x0"], 1)
                        need(dve, S["x0"], j + 1)
                        v.tensor_tensor(xc, xc, y0[:], ALU.add).then_inc(S["x"], 1)
                sweep(dve, CHUNKS, 3, 2, step, 4)



def rank_block(nc, g, io):
    with ExitStack() as stack:
        m = Mem(nc, stack, "rank", g)
        wrt = m.sb("wrt", [PARTS, D])
        xn = m.sb("xn", [PARTS, 2, CTOK])
        dots = m.sb("dots", [PARTS, 2, CTOK])
        score = m.sb("score", [PARTS, TILES])
        rows = m.sb("rows", [PARTS, SEQ])
        ahead, same = m.sb("ahead", [PARTS, SEQ, SEQ]), m.sb("same", [PARTS, SEQ, SEQ])
        tri = m.sb("tri", [PARTS, SEQ, SEQ])
        rank = m.sb("rank", [PARTS, SEQ])
        sig, wgt = m.sb("sig", [PARTS, SEQ]), m.sb("wgt", [PARTS, SEQ])
        p_r = m.ps("p_r", [PARTS, 512])
        p_w = m.ps("p_w", [PARTS, 512])
        S = {n: m.sem(n) for n in ("weights_in", "xn", "dots", "score", "rows_done", "rows", "sig",
                                   "step", "weights", "turned", "kept")}
        with nc.Block() as block:
            @block.sync
            def _(sp):
                m.clear_old(sp)
                sp.dma_start(wrt[:], io["mod_wr"]).then_inc(S["weights_in"], 16)
                sp.dma_start(tri[:], io["earlier"]).then_inc(S["weights_in"], 16)
                sp.wait_ge(S["weights_in"], 32)

            @block.gpsimd
            def _(pool):
                pool.wait_ge(S["weights_in"], 32)

                def step(k, par):
                    need(pool, S["xn"], PER_CHUNK * (k + 1))
                    need(pool, S["score"], k - 1)
                    nc.gpsimd.tensor_tensor(
                        dots[:, par, :].rearrange("p (u d) -> p u d", d=D),
                        xn[:, par, :].rearrange("p (u d) -> p u d", d=D),
                        bc(wrt[:].rearrange("p (o d) -> p o d", o=1), PARTS, PER_CHUNK, D),
                        ALU.mult).then_inc(S["dots"], 1)
                sweep(pool, CHUNKS, 0, 0, step)

            @block.vector
            def _(dve):
                v = nc.vector

                def step(k, par):
                    n = k + 1
                    if inside(n, CHUNKS):
                        need(dve, S["dots"], n - 1)
                        norm_chunk(nc, g, xn[:, 1 - par, :], n, S["xn"])
                    if inside(k, CHUNKS):
                        need(dve, S["dots"], k + 1)
                        v.tensor_reduce(score[:, bass.ts(k, PER_CHUNK)],
                                        dots[:, par, :].rearrange("p (u d) -> p u d", d=D),
                                        AX.X, ALU.add).then_inc(S["score"], 1)
                sweep(dve, CHUNKS, 1, 0, step)
                dve.wait_ge(S["rows_done"], 1)
                v.tensor_copy(rows[:], p_r[:, 0:SEQ]).then_inc(S["rows"], 1)
                dve.wait_ge(S["rows"], 1)
                dve.wait_ge(S["weights_in"], 32)
                own = bc(rows[:].rearrange("p (s o) -> p s o", o=1), PARTS, SEQ, SEQ)
                others = bc(rows[:].rearrange("p (o s) -> p o s", o=1), PARTS, SEQ, SEQ)
                v.tensor_tensor(ahead[:], others, own, ALU.is_gt).then_inc(S["step"], 1)
                v.tensor_tensor(same[:], others, own, ALU.is_equal).then_inc(S["step"], 1)
                dve.wait_ge(S["step"], 2)
                v.tensor_tensor(same[:], same[:], tri[:], ALU.mult).then_inc(S["step"], 1)
                dve.wait_ge(S["step"], 3)
                v.tensor_tensor(ahead[:], ahead[:], same[:], ALU.add).then_inc(S["step"], 1)
                dve.wait_ge(S["step"], 4)
                v.tensor_reduce(rank[:], ahead[:], AX.X, ALU.add).then_inc(S["step"], 1)
                dve.wait_ge(S["step"], 5)
                dve.wait_ge(S["sig"], 1)
                v.scalar_tensor_tensor(wgt[:], rank[:], float(KEPT), sig[:], ALU.is_lt, ALU.mult
                                       ).then_inc(S["weights"], 1)
                dve.wait_ge(S["turned"], 1)
                v.tensor_copy(g.weight[:], p_w[:, 0:TILES]).then_inc(S["kept"], 1)

            @block.scalar
            def _(act):
                act.wait_ge(S["rows"], 1)
                nc.scalar.activation(sig[:], rows[:], ACT.Sigmoid).then_inc(S["sig"], 1)

            @block.tensor
            def _(pe):
                pe.wait_ge(S["score"], CHUNKS)
                for b in range(2):
                    half = slice(64 * b, 64 * b + 64)
                    last = nc.tensor.matmul(p_r[half, 0:SEQ], score[:],
                                            g.const[:, C_ID + 64 * b:C_ID + 64 * b + 64],
                                            start=True, stop=True, skip_group_check=True)
                last.then_inc(S["rows_done"], 1)
                pe.wait_ge(S["weights"], 1)
                for b in range(2):
                    half = slice(64 * b, 64 * b + 64)
                    last = nc.tensor.matmul(p_w[half, 0:TILES], wgt[half, :],
                                            g.const[half, C_ID + 64 * b:C_ID + 64 * b + 64],
                                            start=True, stop=True, skip_group_check=True)
                last.then_inc(S["turned"], 1)


def depths_block(nc, g, io, out):
    with ExitStack() as stack:
        m = Mem(nc, stack, "mod", g)
        NF = FF // PARTS
        w1 = m.sb("w1", [PARTS, FF])
        b1 = m.sb("b1", [PARTS, NF])
        w2 = m.sb("w2", [PARTS, NF, D])
        b2 = m.sb("b2", [PARTS, D])
        xn = m.sb("xn", [PARTS, 2, CTOK])
        xt = m.sb("xt", [PARTS, 2, CTOK])
        gel = m.sb("gel", [PARTS, 2, NF, CTOK])
        xs = m.sb("xs", [PARTS, 2, CTOK])
        y = m.sb("y", [PARTS, 2, CTOK])
        res = m.sb("res", [PARTS, 2, CTOK])
        p_t = m.ps("p_t", [PARTS, 2, CTOK])
        p_h = m.ps("p_h", [PARTS, NF, CTOK])
        p_y = m.ps("p_y", [PARTS, 2, CTOK])
        S = {n: m.sem(n) for n in ("weights_in", "xn", "transposed", "xt", "hidden", "gelu",
                                   "out", "sum", "biased", "res")}
        stored = [m.sem(f"stored{n}") for n in range(2)]
        loads = ((w1, "mod_w1"), (b1, "mod_b1"), (w2, "mod_w2"), (b2, "mod_b2"))
        tiles = lambda a: a.rearrange("p (u d) -> p u d", d=D)
        with nc.Block() as block:
            @block.sync
            def _(sp):
                m.clear_old(sp)
                for to, name in loads:
                    sp.dma_start(to[:], io[name]).then_inc(S["weights_in"], 16)

                def step(k, par):
                    need(sp, S["res"], k + 1)
                    sp.dma_start(out[:, bass.ts(k, PER_CHUNK), :], tiles(res[:, par, :])
                                 ).then_inc(stored[par], 16)
                sweep(sp, CHUNKS, 0, 0, step)
                for par in range(2):
                    sp.wait_ge(stored[par], 16 * CHUNKS // 2)

            @block.tensor
            def _(pe):
                mm = nc.tensor.matmul
                pe.wait_ge(S["weights_in"], 16 * len(loads))

                def step(k, par):
                    n = k + 1
                    if inside(n, CHUNKS):
                        need(pe, S["xn"], PER_CHUNK * (n + 1))
                        need(pe, S["xt"], n - 1)
                        for u in range(PER_CHUNK):
                            last = nc.tensor.transpose(p_t[:, 1 - par, u * D:(u + 1) * D],
                                                       xn[:, 1 - par, u * D:(u + 1) * D],
                                                       g.const[:, C_ID:C_ID + 128])
                        last.then_inc(S["transposed"], 1)
                    if inside(k, CHUNKS):
                        need(pe, S["xt"], k + 1)
                        for f in range(NF):
                            need(pe, S["gelu"], (k - 1) * NF + f + 1)
                            mm(p_h[:, f, :], w1[:, f * PARTS:(f + 1) * PARTS], xt[:, par, :],
                               start=True, stop=True).then_inc(S["hidden"], 1)
                    j = k - 1
                    if inside(j, CHUNKS):
                        need(pe, S["gelu"], (j + 1) * NF)
                        need(pe, S["biased"], j - 1)
                        for u in range(PER_CHUNK):
                            for f in range(NF):
                                last = mm(p_y[:, 1 - par, u * D:(u + 1) * D],
                                          gel[:, 1 - par, f, u * D:(u + 1) * D], w2[:, f, :],
                                          start=(f == 0), stop=(f == NF - 1))
                        last.then_inc(S["out"], 1)
                sweep(pe, CHUNKS, 1, 1, step)

            @block.scalar
            def _(act):
                act.wait_ge(S["weights_in"], 16 * len(loads))

                def step(k, par):
                    n = k + 1
                    if inside(n, CHUNKS):
                        need(act, S["transposed"], n + 1)
                        need(act, S["hidden"], NF * (n - 1))
                        nc.scalar.copy(xt[:, 1 - par, :], p_t[:, 1 - par, :]).then_inc(S["xt"], 1)
                    if inside(k, CHUNKS):
                        need(act, S["out"], k - 1)
                        for f in range(NF):
                            need(act, S["hidden"], k * NF + f + 1)
                            nc.scalar.activation(gel[:, par, f, :], p_h[:, f, :],
                                                 ACT.Gelu_apprx_tanh, bias=b1[:, f:f + 1]
                                                 ).then_inc(S["gelu"], 1)
                sweep(act, CHUNKS, 1, 0, step)

            @block.gpsimd
            def _(pool):
                def step(k, par):
                    need(pool, S["xn"], PER_CHUNK * (k + 1))
                    need(pool, S["res"], k - 1)
                    nc.gpsimd.tensor_tensor(
                        tiles(xs[:, par, :]), g.x[:, bass.ts(k, PER_CHUNK), :],
                        tiles(xn[:, par, :]), ALU.add).then_inc(S["sum"], 1)
                sweep(pool, CHUNKS, 0, 0, step)

            @block.vector
            def _(dve):
                v = nc.vector
                dve.wait_ge(S["weights_in"], 16 * len(loads))

                def step(k, par):
                    n = k + 2
                    if inside(n, CHUNKS):
                        need(dve, S["transposed"], n - 1)
                        need(dve, S["sum"], n - 1)
                        norm_chunk(nc, g, xn[:, par, :], n, S["xn"])
                    j = k - 1
                    if inside(j, CHUNKS):
                        need(dve, S["out"], j + 1)
                        v.tensor_tensor(tiles(y[:, 1 - par, :]), tiles(p_y[:, 1 - par, :]),
                                        bc(b2[:].rearrange("p (o d) -> p o d", o=1),
                                           PARTS, PER_CHUNK, D), ALU.add).then_inc(S["biased"], 1)
                        need(dve, S["biased"], j + 1)
                        need(dve, S["sum"], j + 1)
                        need(dve, stored[1 - par], (j - (1 - par)) * 8)
                        for u in range(PER_CHUNK):
                            cols = slice(u * D, (u + 1) * D)
                            last = v.scalar_tensor_tensor(
                                res[:, 1 - par, cols], y[:, 1 - par, cols],
                                g.weight[:, bass.ds(j * PER_CHUNK + u, 1)], xs[:, 1 - par, cols],
                                ALU.mult, ALU.add)
                        last.then_inc(S["res"], 1)
                sweep(dve, CHUNKS, 2, 1, step)


class Globals:
    pass


def program(nc, io, out, stages=99):
    with ExitStack() as stack:
        m = Mem(nc, stack, "g")
        g = Globals()
        g.sems = []
        g.x = m.sb("x", [PARTS, TILES, D])
        g.const = m.sb("const", [PARTS, C_END])
        g.swap, g.neg = m.sb("swap", [PARTS, PARTS], BF16), m.sb("neg", [PARTS, PARTS], BF16)
        g.delta = m.sb("delta", [PARTS, 32], BF16)
        g.stat = m.sb("stat", [PARTS, TILES, 6])
        g.mean, g.rstd = m.sb("mean", [PARTS, TILES]), m.sb("rstd", [PARTS, TILES])
        load_block(nc, g, io)

        with ExitStack() as attention:
            a = Mem(nc, attention, "attn")
            g.qt, g.kt = a.sb("qt", [PARTS, BATCH * SEQ]), a.sb("kt", [PARTS, BATCH * SEQ])
            g.v2 = a.sb("v2", [PARTS, BATCH, D // 2])
            g.bias_dram = nc.dram_tensor("bias_scratch", (PARTS, 2 * PAIRS, BATCH, SEQ // 2), F32).ap()
            norm_block(nc, g, "norm0")
            project_block(nc, g, io, "proj0", "a0_wq", "a0_wk", "a0_wv")
            bias_block(nc, g, io)
            core_block(nc, g, io, "core0", wo="a0_wo", bias=True)
            if stages > 1:
                norm_block(nc, g, "norm1")
                project_block(nc, g, io, "proj1")
                core_block(nc, g, io, "core1")
        if stages > 2:
            norm_block(nc, g, "norm2")
            experts_block(nc, g, io)
        if stages > 3:
            norm_block(nc, g, "norm3")
            memory_block(nc, g, io)
        if stages > 4:
            with ExitStack() as attention:
                a = Mem(nc, attention, "attn1")
                g.qt, g.kt = a.sb("qt", [PARTS, BATCH * SEQ]), a.sb("kt", [PARTS, BATCH * SEQ])
                g.v2 = a.sb("v2", [PARTS, BATCH, D // 2])
                norm_block(nc, g, "norm4")
                project_block(nc, g, io, "proj4", "a1_wq", "a1_wk", "a1_wv", ctx=True)
                core_block(nc, g, io, "core4", wo="a1_wo", bo="a1_bo", mask="mask")
        if stages > 5:
            g.weight = m.sb("weight", [PARTS, TILES])
            norm_block(nc, g, "norm5")
            rank_block(nc, g, io)
            depths_block(nc, g, io, out)
            return
        store_block(nc, g, out)


def store_block(nc, g, out):
    with ExitStack() as stack:
        m = Mem(nc, stack, "store", g)
        s_out = m.sem("out_stored")
        with nc.Block() as block:
            @block.sync
            def _(sp):
                m.clear_old(sp)
                sp.dma_start(out, g.x[:]).then_inc(s_out, 16)
                sp.wait_ge(s_out, 16)



def arrays_of(inp):
    f = {k: np.asarray(v) for k, v in inp.items()}
    x, ctx, mask = f["x"], f["ctx_1024"], f["mask_Bx1xSxS2_ik1"]
    a = {"x": x.reshape(TILES, PARTS, D).transpose(1, 0, 2), "const": constants()}
    a["ctx_t"] = ctx.reshape(BATCH * SEQ, D).T
    a["ctx_v"] = ctx.reshape(BATCH, SEQ, PAIRS, 2, DH).transpose(3, 1, 0, 2, 4).reshape(
        2, SEQ, BATCH, D // 2)
    keys = mask.reshape(BATCH, SEQ, SEQ).transpose(2, 0, 1)
    a["mask"] = np.concatenate([keys, keys])
    rel = np.zeros((HEADS, DH, PAIRS, 2, REL), np.float32)
    for h in range(HEADS):
        rel[h, :, h // 2, h % 2, :] = f["L0_attn_rel_emb"][:REL].T
    a["rel"] = rel.reshape(PARTS, PAIRS, 2, REL)
    for n, k in (("a0_wq", "L0_attn_Wq"), ("a0_wk", "L0_attn_Wk"), ("a0_wv", "L0_attn_Wv"),
                 ("a0_wo", "L0_attn_Wo"), ("a1_wq", "L1_xattn_wq"), ("a1_wk", "L1_xattn_wk"),
                 ("a1_wv", "L1_xattn_wv"), ("a1_wo", "L1_xattn_wo")):
        a[n] = f[k]
    blocks = lambda w: w.reshape(2, PARTS, -1).transpose(1, 0, 2)
    a["moe_w1t"] = np.stack([blocks(w.T) for w in f["L0_ffn_W1"]], 1)
    a["moe_w2"] = np.stack([blocks(w) for w in f["L0_ffn_W2"]], 1)
    a["moe_w3"] = np.stack([blocks(w) for w in f["L0_ffn_W3"]], 1)
    a["moe_b1"] = f["L0_ffn_b1"].reshape(EXPERTS, 2, PARTS).transpose(2, 0, 1)
    a["moe_b2"] = f["L0_ffn_b2"].reshape(EXPERTS * 2, PARTS).T
    a["moe_b3"] = f["L0_ffn_b3"]
    a["mem_wo"] = f["L1_attn_W_omega"].T
    a["mem_ls"], a["mem_bo"] = f["L1_attn_log_scale"].reshape(D, 1), f["L1_attn_b_omega"].reshape(D, 1)
    a["mem_gamma"] = f["L1_attn_ln_gamma"].reshape(4, D).T
    a["mem_beta"] = f["L1_attn_ln_beta"].reshape(4, D).T
    a["mem_w1"] = f["L1_attn_W1"].T.reshape(4, D, 2 * D).transpose(1, 0, 2)
    a["mem_b1"] = f["L1_attn_b1"].reshape(2, D).T
    a["mem_w2"] = f["L1_attn_W2"].T.reshape(2, D, D).transpose(1, 0, 2)
    a["mem_b2"] = np.tile(f["L1_attn_b2"], (PARTS, 1))
    a["mod_wr"] = np.tile(f["L1_ffn_w_router"], (PARTS, 1))
    a["earlier"] = np.tile(np.tril(np.ones((1, SEQ, SEQ), np.float32), -1), (PARTS, 1, 1))
    a["mod_w1"] = f["L1_ffn_W1"]
    a["mod_b1"] = f["L1_ffn_b1"].reshape(FF // PARTS, PARTS).T
    a["mod_w2"] = f["L1_ffn_W2"].reshape(FF // PARTS, PARTS, D).transpose(1, 0, 2)
    a["mod_b2"] = np.tile(f["L1_ffn_b2"], (PARTS, 1))
    a["moe_wr"] = f["L0_ffn_Wr"]
    a["moe_br"] = np.tile(f["L0_ffn_br"], (PARTS, 1))
    a["a1_bo"] = f["L1_xattn_bo"].reshape(1, D)
    return {k: np.ascontiguousarray(v) for k, v in a.items()}


def kernel(**inputs):
    import concourse.bacc as bacc
    from concourse.bass_utils import run_bass_kernel_spmd

    nc = bacc.Bacc("TRN2", target_bir_lowering=False, num_devices=1)
    arrays = arrays_of(inputs)
    io = {k: nc.dram_tensor(f"in_{k}", v.shape, mybir.dt.from_np(v.dtype), kind="ExternalInput").ap()
          for k, v in arrays.items()}
    out = nc.dram_tensor("out_x", (PARTS, TILES, D), F32, kind="ExternalOutput").ap()
    program(nc, io, out)
    r = run_bass_kernel_spmd(nc, [{f"in_{k}": v for k, v in arrays.items()}], core_ids=[0])
    got = r.results[0]["out_x"]
    return np.ascontiguousarray(got.transpose(1, 0, 2)).reshape(BATCH, SEQ, D)
```
